# Optimizing a Trainium2 kernel written in Bass

```python
import numpy as np
import jax
import jax.numpy as jnp

def _softmax(x, axis=-1):
    return jax.nn.softmax(x, axis=axis)
def _gelu(x):
    return jax.nn.gelu(x, approximate=True)
def _silu(x):
    return jax.nn.silu(x)
def _sigmoid(x):
    return jax.nn.sigmoid(x)
def _layernorm(x, axis=-1, eps=1e-5):
    m = jnp.mean(x, axis=axis, keepdims=True)
    v = jnp.var(x, axis=axis, keepdims=True)
    return (x - m) / jnp.sqrt(v + eps)
def _scatter_add(tgt, idx, src, axis=0):
    return tgt.at[idx].add(src)
def _segment_sum(src, seg, n):
    return jax.ops.segment_sum(src, seg, n)

kernel_name = 'mk_conv_preact_d2_conv_nchw384_ee4bc8'

def setup_inputs(seed: int = 0):
    np.random.seed(seed)
    _w = jnp.asarray
    def _rec_inputs():
        import jax
        import jax.numpy as jnp
        _gk = jax.random.key(seed)
        x = -0.0001538 + 1 * jax.random.normal(jax.random.fold_in(_gk, 1), (16, 384, 32, 32), jnp.float32)
        return x
    x = _rec_inputs()
    def _L0_conv_setup():
        import jax, jax.numpy as jnp
        import numpy as np
        DIM = 384
        DIM_HEAD = 32
        NUM_HEAD = DIM // DIM_HEAD
        SCALE = DIM_HEAD ** (-0.5)
        key = jax.random.key(seed)
        k1, k2, k3, k4 = jax.random.split(key, 4)
        x = jax.random.normal(k1, (16, DIM, 32, 32), dtype=jnp.float32)
        qkv_w = jax.random.normal(k2, (3 * DIM, DIM), dtype=jnp.float32) * DIM ** (-0.5)
        proj_w = jax.random.normal(k3, (DIM, DIM), dtype=jnp.float32) * DIM ** (-0.5)
        proj_b = jax.random.normal(k4, (DIM,), dtype=jnp.float32) * 0.01
        return {'x': x, 'qkv_w': qkv_w, 'proj_w': proj_w, 'proj_b': proj_b}
    _L0_conv_all = _L0_conv_setup()
    _L0_conv_in = {k: v for k, v in _L0_conv_all.items() if k in ('qkv_w', 'proj_w', 'proj_b', )}
    del _L0_conv_all

    def _L1_conv_setup():
        import jax, jax.numpy as jnp
        import numpy as np
        HEADS = 8
        HEAD_DIM = 48
        FOLD = 2
        PROP = 4
        EPS = 1e-12

        def _fold(t, f):
            b, c, Wd, Hd = t.shape
            w, h = (Wd // f, Hd // f)
            t = t.reshape(b, c, f, w, f, h).transpose(0, 2, 4, 1, 3, 5)
            return t.reshape(b * f * f, c, w, h)

        def _unfold(t, f):
            bff, c, w, h = t.shape
            b = bff // (f * f)
            t = t.reshape(b, f, f, c, w, h).transpose(0, 3, 1, 4, 2, 5)
            return t.reshape(b, c, f * w, f * h)

        def _adaptive_avg_pool(t, pw, ph):
            b, c, w, h = t.shape
            return t.reshape(b, c, pw, w // pw, ph, h // ph).mean(axis=(3, 5))
        key = jax.random.key(seed)
        ks = jax.random.split(key, 6)
        B, C, H, W = (32, 384, 56, 56)
        D = HEADS * HEAD_DIM
        return {'x': jax.random.normal(ks[0], (B, C, H, W), jnp.float32), 'Wf': jax.random.normal(ks[1], (D, C), jnp.float32) * 0.02, 'bf': jnp.zeros((D,), jnp.float32), 'Wv': jax.random.normal(ks[2], (D, C), jnp.float32) * 0.02, 'bv': jnp.zeros((D,), jnp.float32), 'Wp': jax.random.normal(ks[3], (C, D), jnp.float32) * 0.02, 'bp': jnp.zeros((C,), jnp.float32), 'sim_alpha': jnp.ones((1,), jnp.float32), 'sim_beta': jnp.zeros((1,), jnp.float32)}
    _L1_conv_all = _L1_conv_setup()
    _L1_conv_in = {k: v for k, v in _L1_conv_all.items() if k in ('Wf', 'bf', 'Wv', 'bv', 'Wp', 'bp', 'sim_alpha', 'sim_beta', )}
    del _L1_conv_all

    return {
        "x": x,
        "L0_conv_qkv_w": _L0_conv_in["qkv_w"],
        "L0_conv_proj_w": _L0_conv_in["proj_w"],
        "L0_conv_proj_b": _L0_conv_in["proj_b"],
        "L1_conv_Wf": _L1_conv_in["Wf"],
        "L1_conv_bf": _L1_conv_in["bf"],
        "L1_conv_Wv": _L1_conv_in["Wv"],
        "L1_conv_bv": _L1_conv_in["bv"],
        "L1_conv_Wp": _L1_conv_in["Wp"],
        "L1_conv_bp": _L1_conv_in["bp"],
        "L1_conv_sim_alpha": _L1_conv_in["sim_alpha"],
        "L1_conv_sim_beta": _L1_conv_in["sim_beta"],
    }

def reference(x, L0_conv_qkv_w, L0_conv_proj_w, L0_conv_proj_b, L1_conv_Wf, L1_conv_bf, L1_conv_Wv, L1_conv_bv, L1_conv_Wp, L1_conv_bp, L1_conv_sim_alpha, L1_conv_sim_beta):
    import jax
    import jax.numpy as jnp
    def _L0_conv_ref(x, qkv_w, proj_w, proj_b):
        import jax, jax.numpy as jnp
        import numpy as np
        DIM = 384
        DIM_HEAD = 32
        NUM_HEAD = DIM // DIM_HEAD
        SCALE = DIM_HEAD ** (-0.5)
        B, C, H, W = x.shape
        N = H * W
        xt = x.reshape(B, C, N).transpose(0, 2, 1)
        qkv = jnp.einsum('bnc,oc->bno', xt, qkv_w)
        qkv = qkv.reshape(B, N, 3, NUM_HEAD, DIM_HEAD).transpose(2, 0, 3, 1, 4)
        q, k, v = (qkv[0], qkv[1], qkv[2])
        attn = jnp.einsum('bhnd,bhmd->bhnm', q, k) * SCALE
        attn = jax.nn.softmax(attn, axis=-1)
        out = jnp.einsum('bhnm,bhmd->bhnd', attn, v)
        out = out.transpose(0, 2, 1, 3).reshape(B, N, C)
        out = jnp.einsum('bnc,oc->bno', out, proj_w) + proj_b
        return out.transpose(0, 2, 1).reshape(B, C, H, W)

    def _L1_conv_ref(x, Wf, bf, Wv, bv, Wp, bp, sim_alpha, sim_beta):
        import jax, jax.numpy as jnp
        import numpy as np
        HEADS = 8
        HEAD_DIM = 48
        FOLD = 2
        PROP = 4
        EPS = 1e-12

        def _fold(t, f):
            b, c, Wd, Hd = t.shape
            w, h = (Wd // f, Hd // f)
            t = t.reshape(b, c, f, w, f, h).transpose(0, 2, 4, 1, 3, 5)
            return t.reshape(b * f * f, c, w, h)

        def _unfold(t, f):
            bff, c, w, h = t.shape
            b = bff // (f * f)
            t = t.reshape(b, f, f, c, w, h).transpose(0, 3, 1, 4, 2, 5)
            return t.reshape(b, c, f * w, f * h)

        def _adaptive_avg_pool(t, pw, ph):
            b, c, w, h = t.shape
            return t.reshape(b, c, pw, w // pw, ph, h // ph).mean(axis=(3, 5))
        v = jnp.einsum('bchw,dc->bdhw', x, Wv) + bv[None, :, None, None]
        f = jnp.einsum('bchw,dc->bdhw', x, Wf) + bf[None, :, None, None]

        def split_heads(t):
            b, d, w, h = t.shape
            return t.reshape(b * HEADS, d // HEADS, w, h)
        f = _fold(split_heads(f), FOLD)
        v = _fold(split_heads(v), FOLD)
        b, c, w, h = f.shape
        centers = _adaptive_avg_pool(f, PROP, PROP)
        vc = _adaptive_avg_pool(v, PROP, PROP).reshape(b, c, -1).transpose(0, 2, 1)
        cen = centers.reshape(b, c, -1).transpose(0, 2, 1)
        tok = f.reshape(b, c, -1).transpose(0, 2, 1)
        cen_n = cen / jnp.maximum(jnp.linalg.norm(cen, axis=-1, keepdims=True), EPS)
        tok_n = tok / jnp.maximum(jnp.linalg.norm(tok, axis=-1, keepdims=True), EPS)
        sim = jax.nn.sigmoid(sim_beta + sim_alpha * jnp.einsum('bmc,bnc->bmn', cen_n, tok_n))
        idx = jnp.argmax(sim, axis=1)
        mask = jax.nn.one_hot(idx, sim.shape[1], dtype=sim.dtype).transpose(0, 2, 1)
        sim = sim * mask
        v2 = v.reshape(b, c, -1).transpose(0, 2, 1)
        agg = (jnp.einsum('bmn,bnc->bmc', sim, v2) + vc) / (sim.sum(-1, keepdims=True) + 1.0)
        out = jnp.einsum('bmn,bmc->bnc', sim, agg)
        out = out.transpose(0, 2, 1).reshape(b, c, w, h)
        out = _unfold(out, FOLD)
        be, _, W2, H2 = out.shape
        out = out.reshape(be // HEADS, HEADS * c, W2, H2)
        out = jnp.einsum('bdhw,od->bohw', out, Wp) + bp[None, :, None, None]
        return out

    def _gn(v, G=32, eps=1e-5):
        B_, C_, H_, W_ = v.shape
        g = v.reshape(B_, G, C_ // G, H_, W_)
        m = jnp.mean(g, axis=(2, 3, 4), keepdims=True)
        s = jnp.var(g, axis=(2, 3, 4), keepdims=True)
        return ((g - m) / jnp.sqrt(s + eps)).reshape(v.shape)

    def _ln_c(v, eps=1e-6):
        m = jnp.mean(v, axis=1, keepdims=True)
        s = jnp.var(v, axis=1, keepdims=True)
        return (v - m) / jnp.sqrt(s + eps)

    def _ln_t(v, eps=1e-5):
        m = jnp.mean(v, axis=-1, keepdims=True)
        s = jnp.var(v, axis=-1, keepdims=True)
        return (v - m) / jnp.sqrt(s + eps)

    def _to_tokens(v):
        B_, C_, H_, W_ = v.shape
        return v.reshape(B_, C_, H_ * W_).transpose(0, 2, 1)
    def _from_tokens(t, like):
        B_, C_, H_, W_ = like.shape
        return t.transpose(0, 2, 1).reshape(B_, C_, H_, W_)

    x = x + _L0_conv_ref(_gn(x), L0_conv_qkv_w, L0_conv_proj_w, L0_conv_proj_b)
    x = x + _L1_conv_ref(_gn(x), L1_conv_Wf, L1_conv_bf, L1_conv_Wv, L1_conv_bv, L1_conv_Wp, L1_conv_bp, L1_conv_sim_alpha, L1_conv_sim_beta)
    return x


_drawn_inputs = setup_inputs


def setup_inputs(seed=0):
    import zlib

    import numpy as np

    out = dict(_drawn_inputs(seed))
    spreads = {'L1_conv_bf': (0.0, 0.768), 'L1_conv_bv': (0.0, 0.342), 'L1_conv_bp': (0.0, 0.1)}
    factors = {'L0_conv_proj_b': 6.136, 'L1_conv_Wf': 2.702}
    for name, (base, spread) in spreads.items():
        noise = np.random.default_rng([zlib.crc32(name.encode()), seed]).standard_normal(out[name].shape)
        drawn = base * np.exp(spread * noise) if base else spread * noise
        out[name] = jnp.asarray(drawn.astype(out[name].dtype))
    for name, factor in factors.items():
        out[name] = (out[name] * factor).astype(out[name].dtype)
    return out
```

```python
from contextlib import ExitStack

import concourse.bass as bass
from concourse import mybir

P = 128
C, KC = 384, 3
N = 1024
HEADS0, DH0 = 12, 32
GROUPS, HPG = 3, 4
HEADS1, DH1 = 8, 48
QUADS, QT = 4, 256
CENT = 16
HM = HEADS1 * CENT
STEPS = 16
SCALE0 = float(DH0) ** -0.5
GN_GROUPS, GN_EPS = 32, 1e-5
NORM_EPS2 = 1e-24
VW = C + 1
KROWS = 98

C_ID, C_GA, C_BD, C_MD, C_SEL, C_W16, C_ONE, C_NH = 0, 128, 224, 608, 632, 1144, 1160, 1288
C_COLS = 1289



QK_STEPS = (5, 7, 8, 10, 11, 13, 14, 15)


def work_items():
    at = [[] for _ in range(GROUPS * STEPS + 1)]
    spread = [0, 0, 4, 5, 4, 6, 4, 5, 4, 5, 4, 5, 4, 5, 4, 5]
    last = [0, 0, 2, 3, 2, 3, 2, 3, 2, 3, 2, 3, 2, 3, 2, 0]
    for g in range(GROUPS):
        m = 0
        for s in range(STEPS):
            n = (last if g == GROUPS - 1 else spread)[s]
            at[g * STEPS + s] += [("max", m + i) for i in range(n)]
            m += n
            if s == (15 if g == GROUPS - 1 else 10):
                at[g * STEPS + s].append(("nm", 0))
            if s in QK_STEPS:
                at[g * STEPS + s].append(("qk", QK_STEPS.index(s)))
        assert m == (32 if g == GROUPS - 1 else 64)
        if g < GROUPS - 1:
            at[(g + 1) * STEPS + 1].append(("nm", 1))
    at[9].append(("gs1", 0))
    at[12].append(("gs2", 0))
    return at


WORK = work_items()
LATE_WORK, tile = {}, 32
for after, n in ((("vp", 0), 2), (("vp", 1), 2), (("vp", 2), 2), (("vp", 3), 2), (("vp", 4), 2), (("proj", 0), 1),
                 (("proj", 1), 1), (("proj", 2), 1), (("proj", 3), 1), (("proj", 4), 1), (("proj", 5), 1),
                 (("gs1", 0), 4), (("vp", 6), 2), (("gs2", 0), 5), (("vc", 0), 5)):
    LATE_WORK[after] = [("max", tile + i) for i in range(n)]
    tile += n
assert tile == 64
LATE_WORK["f", 1] = [("nm", 1)]
WORK_N = sum(map(len, WORK)) + sum(map(len, LATE_WORK.values()))
PRE_WORK = ([("gs1", 0), ("gs2", 0)] + [("qk", c) for c in range(8)] + [("v", t) for t in range(8)]
            + [("max", m) for m in range(32)] + [("nm", 0)] + [("max", m) for m in range(32, 64)]
            + [("nm", 1)] + [("qk1", c) for c in range(8)])
PRE_N = len(PRE_WORK)
assert WORK_N % 2 == 0 and PRE_N % 2 == 0


def layer1_items():
    out = [("vp", i, 2 + i % 2, "A") for i in range(5)]
    out += [("proj", i, (0, 1, 6, 7, 0, 1)[i], "D") for i in range(6)]
    out += [("gs1", 0, 6, "D"), ("vp", 5, 3, "A"), ("vp", 6, 2, "A"), ("gs2", 0, 7, "D"), ("vp", 7, 3, "A")]
    out += [("cen", 0, 6, "D"), ("vc", 0, 7, "A")]
    for t in range(8):
        out += [("f", t, t % 2, "A"), ("v", t, 6 + t % 2, "D")]
        if t == 2:
            out += [("cenT", 0, 2, "D")]
        if t == 4:
            out += [("gc", 0, 3, "D")]
        if t in (5, 6, 7):
            out += [("G", t - 5, 2 + (t - 5) % 2, "A")]
    out += [("num", 0, 0, "D"), ("num", 1, 1, "D"), ("agg", 0, 2, "D"), ("sT", 0, 6, "A")]
    for q in range(QUADS):
        out += [("aT", q, 6 + q % 2, "A")]
        if q + 2 < QUADS:
            out += [("num", q + 2, q % 2, "D")]
        out += [("MT", q, 2 + q % 2, "A")]
        if q + 1 < QUADS:
            out += [("agg", q + 1, 2 + (q + 1) % 2, "D")]
        out += [("outa", q, 0, "D"), ("outb", q, 1, "D")]
        if q + 1 < QUADS:
            out += [("sT", q + 1, 6 + (q + 1) % 2, "A")]
    return out


L1 = layer1_items()
L1_AT = {(k, i): n for n, (k, i, _, _) in enumerate(L1)}
L1_N = len(L1)
L1_D = sum(w == "D" for _, _, _, w in L1)
L1_A = L1_N - L1_D


def freed_before(n):
    bank = L1[n][2]
    for m in range(n - 1, -1, -1):
        if L1[m][2] == bank:
            who = L1[m][3]
            return who, sum(w == who for _, _, _, w in L1[:m + 1])
    return None, 0


def act_items(kind, i):
    return sum(w == "A" for _, _, _, w in L1[:L1_AT[kind, i] + 1])


def conv_kernel(nc, samples, x, qkv_t, proj_t, proj_b, wf_t, wf_n, bf, wv_t, bv, wp_t, bp, alpha, beta, consts, y):
    f32, f32r = mybir.dt.float32, mybir.dt.float32r
    ALU, ACT, AX = mybir.AluOpType, mybir.ActivationFunctionType, mybir.AxisListType
    ctx = ExitStack()
    with ctx:
        def sb(name, shape, dt=f32):
            return ctx.enter_context(nc.sbuf_tensor(name, shape, dt))

        def sem(name):
            return ctx.enter_context(nc.semaphore(name))

        cst = sb("cst", [P, C_COLS])
        ident = cst[:, C_ID:C_ID + P]
        grp_avg = cst[:, C_GA:C_GA + 96].rearrange("p (k g) -> p k g", k=KC)
        mask_hm = cst[:, C_BD:C_BD + C]
        mask_d = cst[:, C_MD:C_MD + 24].rearrange("p (k h) -> p k h", k=KC)
        sel_q = cst[0:64, C_SEL:C_SEL + 512].rearrange("p (q n) -> p q n", q=QUADS)
        grp_back = cst[64:96, C_SEL:C_SEL + C].rearrange("p (k c) -> p k c", k=KC)
        gcr = cst[96:97, C_SEL:C_SEL + 512]
        first_w = cst[:, C_W16:C_W16 + CENT]
        ones = cst[:, C_ONE:C_ONE + P]
        neg_half = cst[:, C_NH:C_NH + 1]
        wqkv = sb("wqkv", [P, KC, 3 * C])
        wproj = sb("wproj", [P, KC, C])
        wf = sb("wf", [P, KC, C])
        wfn = sb("wfn", [P, KC, C])
        wv = sb("wv", [P, KC, C])
        wp = sb("wp", [P, KC, C])
        bvm = sb("bvm", [P, C])
        bfb = sb("bfb", [64, C])
        cols = sb("cols", [P, 16])
        pb_c, bp_c, bf_c = cols[:, 0:3], cols[:, 3:6], cols[:, 6:9]
        nalpha, nbeta = cols[:, 9:10], cols[:, 10:11]
        xs = sb("xs", [P, 2, KC, N])
        xn = sb("xn", [P, KC, N])
        qkn = sb("qkn", [P, 2, 2, N], f32r)
        qs = sb("qs", [P, 2, 2, HPG, 512], f32r)
        ks = sb("ks", [P, 2, HPG, N], f32r)
        vt0 = sb("vt0", [P, 8, C])
        arena = sb("arena", [P, 8192])
        prob = arena[:, 0:6144].rearrange("p (r n) -> p r n", r=6)
        psums = arena[:, 6144:8192].rearrange("p (r n) -> p r n", r=2)
        xn1 = arena[:, 0:3072].rearrange("p (k q n) -> p k q n", k=KC, q=QUADS)
        vt1 = arena[:, 3072:3072 + 8 * VW].rearrange("p (t n) -> p t n", t=8)
        pool1 = arena[:, 3072:3840].rearrange("p (k n) -> p k n", k=KC)
        gmat = arena[:, 6152:6152 + 1536].rearrange("p (k n) -> p k n", k=KC)
        ao = sb("ao", [P, KC, N])
        aof = ao[:, :, :].rearrange("p k n -> p (k n)")
        bdc = aof[:, 0:1536].rearrange("p (k n) -> p k n", k=KC)
        sig = aof[:, 0:256]
        eq = aof[:, 256:512]
        wgt = aof[:, 512:768]
        cosb = aof[:, 768:1024]
        simm = aof[:, 1024:1536].rearrange("p (b n) -> p b n", b=2)
        sq = aof[:, 1536:2304].rearrange("p (b n) -> p b n", b=2)
        agg = aof[:, 1536:1920]
        aggt = aof[:, 1920:2304].rearrange("p (k n) -> p k n", k=KC)
        cen = aof[0:64, 2304:2688]
        csq = aof[0:64, 2688:3072]
        mts = aof[:, 2304:2688]
        simt = aof[:, 2688:2944]
        vcx = sb("vcx", [64, VW])
        rden = sb("rden", [P, 512])
        mx = sb("mx", [P, 2, 16, 2])
        nmx = sb("nmx", [P, 16])
        nmp = sb("nmp", [16, 2, P], f32r)
        st6 = sb("st6", [P, KC, 2, 6])
        mv = sb("mv", [P, KC, 2])
        gst = sb("gst", [P, 8])
        sc0 = sb("sc0", [P, KC, 2])
        sc1 = sb("sc1", [P, KC, 2])
        pxn = sb("pxn", [P, KC, 64])
        cn2 = sb("cn2", [64, 2, HEADS1])
        nsq = sb("nsq", [P, 8, HEADS1])
        rn = sb("rn", [P, 8, HEADS1])
        mxs = sb("mxs", [P, 16])
        mw = sb("mw", [P, 16])
        rs = sb("rs", [P, 1])
        bank = [ctx.enter_context(nc.psum_tensor(f"bank{i}", [P, 2 if i in (0, 2) else 1, 512], f32))
                for i in (0, 2, 4, 5, 6, 7)]
        score = [bank[0], bank[1]]
        work = [bank[2][:, 0, :], bank[3][:, 0, :]]
        obank, dbank = bank[4][:, 0, :], bank[5][:, 0, :]
        lb = {0: bank[0][:, 0, :], 1: bank[0][:, 1, :], 2: bank[1][:, 0, :], 3: bank[1][:, 1, :],
              6: obank, 7: dbank}

        const_in = sem("const_in")
        const_done = sem("const_done")
        x_in = sem("x_in")
        score_ready = sem("score_ready")
        exp_done = sem("exp_done")
        pv_done = sem("pv_done")
        sum_done = sem("sum_done")
        den_done = sem("den_done")
        o_copied = sem("o_copied")
        den_copied = sem("den_copied")
        ao_done = sem("ao_done")
        work_ready = sem("work_ready")
        work_free = sem("work_free")
        qk_hi = sem("qk_hi")
        qk_lo = sem("qk_lo")
        stack_in = [sem(f"stack_in{h}") for h in range(HPG)]
        negmax = sem("negmax")
        nm_ready = sem("nm_ready")
        nm_in = sem("nm_in")
        mv_ready = sem("mv_ready")
        var_ready = sem("var_ready")
        rstd_ready = sem("rstd_ready")
        gb_ready = sem("gb_ready")
        sc_ready = sem("sc_ready")
        xn_ready = sem("xn_ready")
        v0_ready = sem("v0_ready")
        l_ready = sem("l_ready")
        l_act = sem("l_act")
        l_dve = sem("l_dve")
        xn1_ready = sem("xn1_ready")
        pxn_ready = sem("pxn_ready")
        cnorm_ready = sem("cnorm_ready")
        crn_ready = sem("crn_ready")
        cen_ready = sem("cen_ready")
        bd_ready = sem("bd_ready")
        sq_used = sem("sq_used")
        norm_ready = sem("norm_ready")
        rn_ready = sem("rn_ready")
        cos_ready = sem("cos_ready")
        sexp_ready = sem("sexp_ready")
        sim_ready = sem("sim_ready")
        agg_ready = sem("agg_ready")
        y_ready = sem("y_ready")
        y_out = sem("y_out")
        chain = sem("chain")
        block = ctx.enter_context(nc.Block())

        PAIRS = samples // 2
        UNIT_TILES = 2 * STEPS

        def quad_view(ap, q):
            f1, f2 = divmod(q, 2)
            v = ap.rearrange("p (y x) -> p y x", y=32)
            return v[:, 16 * f1:16 * f1 + 16, 16 * f2:16 * f2 + 16]

        @block.sync
        def _(sp):
            def stack(n, buf):
                for h in range(HPG):
                    r = slice(32 * h, 32 * h + 32)
                    q_hi, q_lo = qkn[r, 0, 0, :].bitcast(f32), qkn[r, 0, 1, :].bitcast(f32)
                    k_hi, k_lo = qkn[r, 1, 0, :].bitcast(f32), qkn[r, 1, 1, :].bitcast(f32)
                    for row, src in ((0, k_hi), (32, k_hi), (64, k_lo)):
                        sp.dma_start(ks[row:row + 32, buf, h, :].bitcast(f32), src).then_inc(stack_in[h], 16)
                    for row, src in ((0, q_hi), (32, q_lo), (64, q_hi)):
                        sp.dma_start(qs[row:row + 32, buf, :, h, :].bitcast(f32),
                                     src.rearrange("p (a n) -> p a n", a=2)).then_inc(stack_in[h], 16)

            def maxima(buf, half):
                for part in range(2):
                    dst = qs[96 + part:97 + part, buf, half, :, :].bitcast(f32).rearrange("o h n -> o (h n)")
                    sp.dma_start(dst, nmp[:, part, :].bitcast(f32)).then_inc(nm_in, 16)

            for k in range(KC):
                sp.dma_start(xs[:, 0, k, :], x[0, k * P:k * P + P, :]).then_inc(x_in, 16)
            sp.dma_start(cst[:, :], consts).then_inc(const_in, 16)
            for t, src in ((wqkv, qkv_t), (wproj, proj_t), (wf, wf_t), (wfn, wf_n), (wv, wv_t), (wp, wp_t)):
                sp.dma_start(t[:, :, :], src.rearrange("(k p) n -> p k n", p=P)).then_inc(const_in, 16)
            for k in range(KC):
                sp.dma_start(xs[:, 1, k, :], x[1, k * P:k * P + P, :]).then_inc(x_in, 16)
            for t, src in ((pb_c, proj_b), (bp_c, bp), (bf_c, bf)):
                for k in range(KC):
                    sp.dma_start(t[:, k:k + 1], src[k * P:k * P + P].rearrange("(p o) -> p o", o=1)).then_inc(const_in, 16)
            sp.dma_start(bvm[:, :], bv.rearrange("(o c) -> o c", o=1).to_broadcast((P, C))).then_inc(const_in, 16)
            sp.dma_start(bfb[:, :], bf.rearrange("(o c) -> o c", o=1).to_broadcast((64, C))).then_inc(const_in, 16)
            sp.dma_start(nalpha, alpha.rearrange("(o c) -> o c", o=1).to_broadcast((P, 1))).then_inc(const_in, 16)
            sp.dma_start(nbeta, beta.rearrange("(o c) -> o c", o=1).to_broadcast((P, 1))).then_inc(const_in, 16)

            sp.wait_ge(qk_lo, 8)
            stack(0, 0)
            for half in range(2):
                sp.wait_ge(nm_ready, half + 1)
                maxima(0, half)
            sp.wait_ge(qk_lo, 16)
            stack(1, 1)
            with sp.Fori(0, PAIRS) as it:
                this = [sp.snap(it * 2 + j) for j in range(2)]
                ahead = [sp.snap(it * 2 + (j + 2)) for j in range(2)]
                for j in range(2):
                    def count(per, n):
                        return it * (2 * per) + (j * per + n)
                    for g in range(GROUPS):
                        u = 3 * j + g
                        if g:
                            sp.wait_ge(nm_ready, count(6, 2 * g + 2))
                            maxima(u % 2, 1)
                        sp.wait_ge(nm_ready, count(6, 2 * g + 3))
                        maxima((u + 1) % 2, 0)
                        sp.wait_ge(qk_lo, count(24, 8 * g + 24))
                        stack(u + 2, u % 2)
                    sp.wait_ge(nm_ready, count(6, 8))
                    maxima((3 * j + 3) % 2, 1)
                    sp.wait_ge(y_ready, count(QUADS, QUADS))
                    for k in range(KC):
                        sp.dma_start(y[bass.ds(this[j], 1), k * P:k * P + P, :], xs[:, j, k, :]).then_inc(y_out, 16)
                    sp.wait_ge(y_out, count(16 * KC, 16 * KC))
                    for k in range(KC):
                        sp.dma_start(xs[:, j, k, :], x[bass.ds(ahead[j], 1), k * P:k * P + P, :]).then_inc(x_in, 16)
            sp.wait_ge(x_in, 16 * KC * (samples + 2))
            sp.wait_ge(y_out, 16 * KC * samples)

        @block.tensor
        def _(pe):
            mm = nc.tensor.matmul

            def max_tile(m, buf, out):
                half, h, qt, kh = m // 32, m // 8 % 4, m // 2 % 4, m % 2
                return mm(out, qs[0:96, buf, half, h, qt * P:qt * P + P], ks[0:96, buf, h, kh * 512:kh * 512 + 512],
                          start=True, stop=True)

            def qk_chunk(g, c, out):
                w0 = (c // 4) * C + g * P
                for k in range(KC):
                    last = mm(out[:, 0:256], wqkv[:, k, w0:w0 + P], xn[:, k, (c % 4) * 256:(c % 4) * 256 + 256],
                              start=(k == 0), stop=(k == KC - 1))
                return last

            def value_tile(t, out):
                for k in range(KC):
                    last = mm(out[:, 0:C], xn[:, k, t * P:t * P + P], wqkv[:, k, 2 * C:3 * C],
                              start=(k == 0), stop=(k == KC - 1))
                return last

            def group_stats(out):
                for k in range(KC):
                    last = mm(out[64:96, 0:2], grp_avg[:, k, :], mv[:, k, :], start=(k == 0), stop=(k == KC - 1))
                return last

            def group_back(out):
                for k in range(KC):
                    last = mm(out[:, 2 * k:2 * k + 2], grp_back[:, k, :], gst[64:96, 0:2], start=True, stop=True)
                return last

            def max_rows(out):
                return nc.tensor.transpose(out[0:16, 0:P], nmx[:, :], ident)

            pe.sem_inc(pv_done, 3)
            pe.sem_inc(den_done, 1)
            pe.wait_ge(const_in, 16 * 20)
            pe.wait_ge(const_done, 1)
            for i, (kind, a) in enumerate(PRE_WORK):
                out = work[i % 2]
                pe.wait_ge(work_free, i + 1)
                if kind == "gs1":
                    pe.wait_ge(mv_ready, 1)
                    group_stats(out).then_inc(work_ready, 1)
                elif kind == "gs2":
                    pe.wait_ge(gb_ready, 1)
                    group_back(out).then_inc(work_ready, 1)
                elif kind in ("qk", "qk1"):
                    if a == 0:
                        pe.wait_ge(xn_ready, KC)
                    qk_chunk(kind == "qk1", a, out).then_inc(work_ready, 1)
                elif kind == "v":
                    value_tile(a, out).then_inc(work_ready, 1)
                elif kind == "max":
                    if a in (0, 8, 16, 24):
                        pe.wait_ge(stack_in[a // 8], 96)
                    max_tile(a, 0, out).then_inc(work_ready, 1)
                else:
                    pe.wait_ge(negmax, a + 1)
                    max_rows(out).then_inc(work_ready, 1)

            pe.wait_ge(v0_ready, 8)
            with pe.Fori(0, PAIRS) as it:
                for j in range(2):
                    def count(per, n):
                        return it * (2 * per) + (j * per + n)

                    pe.wait_ge(l_act, count(L1_A, 1 + 0))
                    pe.wait_ge(l_dve, count(L1_D, 1 + 0))
                    done = 0

                    def fill(g, kind, a):
                        nonlocal done
                        i = done
                        done += 1
                        out = work[i % 2]
                        pe.wait_ge(work_free, count(WORK_N, PRE_N + i + 1))
                        if kind == "max":
                            if a in (0, 8, 16, 24):
                                pe.wait_ge(stack_in[a // 8], count(3 * 96, 96 * (g + 2)))
                            max_tile(a, (3 * j + g + 1) % 2, out).then_inc(work_ready, 1)
                        elif kind == "nm":
                            pe.wait_ge(negmax, count(6, 2 * g + 3 if a == 0 else 2 * g + 2))
                            max_rows(out).then_inc(work_ready, 1)
                        elif kind == "qk":
                            if g == 1 and a == 0:
                                pe.wait_ge(xn_ready, count(KC, 2 * KC))
                            qk_chunk((g + 2) % 3, a, out).then_inc(work_ready, 1)
                        elif kind == "gs1":
                            pe.wait_ge(mv_ready, count(2, 2))
                            group_stats(out).then_inc(work_ready, 1)
                        else:
                            pe.wait_ge(gb_ready, count(2, 2))
                            group_back(out).then_inc(work_ready, 1)

                    for S in range(GROUPS * STEPS + 4):
                        g, s = divmod(S, STEPS)
                        half, kb = divmod(s, 8)
                        u = 3 * j + g
                        items = list(WORK[S]) if S < len(WORK) else []

                        def work_item():
                            if items:
                                fill(g, *items.pop(0))

                        for p in range(2):
                            if S < GROUPS * STEPS:
                                t = 2 * S + p
                                if kb == 0 and p == 0:
                                    pe.wait_ge(nm_in, count(6 * 32, 32 * (2 * g + half + 1)))
                                pe.wait_ge(exp_done, count(96, t + 1))
                                for e in range(2):
                                    h = 2 * p + e
                                    last = mm(score[p][:, e, :], ks[0:KROWS, u % 2, h, kb * P:kb * P + P],
                                              qs[0:KROWS, u % 2, half, h, :],
                                              start=True, stop=True)
                                last.then_inc(score_ready, 1)
                            work_item()
                        if 1 <= S <= GROUPS * STEPS:
                            T = S - 1
                            tg, tkb = T // STEPS, T % 8
                            if tkb == 0:
                                pe.wait_ge(o_copied, count(6, 1 + T // 8))
                            pe.wait_ge(exp_done, count(96, 2 * T + 4))
                            for h in range(HPG):
                                r = slice(32 * h, 32 * h + 32)
                                last = mm(obank[r, :], vt0[:, tkb, tg * P + 32 * h:tg * P + 32 * h + 32],
                                          prob[:, (2 * T + h // 2) % 6, (h % 2) * 512:(h % 2) * 512 + 512],
                                          start=(tkb == 0), stop=(tkb == 7))
                            last.then_inc(pv_done, 1)
                        work_item()
                        work_item()
                        if S >= 3 and S % 2 == 1 and (S - 3) // 2 < 24:
                            d = (S - 3) // 2
                            if d % 4 == 0:
                                pe.wait_ge(den_copied, count(6, 1 + d // 4))
                            pe.wait_ge(sum_done, count(48, 2 * d + 6))
                            for h in range(HPG):
                                r = slice(32 * h, 32 * h + 32)
                                last = mm(dbank[r, :], ones[:, 0:32],
                                          psums[:, h // 2, (h % 2) * 512:(h % 2) * 512 + 512],
                                          start=(d % 4 == 0), stop=(d % 4 == 3))
                            last.then_inc(den_done, 1)
                        while len(items) > 0:
                            work_item()
                    pe.wait_ge(exp_done, count(96, 98))
                    for n, (kind, a, bk, who) in enumerate(L1):
                        out = lb[bk]
                        before, freed = freed_before(n)
                        if before == "A":
                            pe.wait_ge(l_act, count(L1_A, 1 + freed))
                        elif before == "D":
                            pe.wait_ge(l_dve, count(L1_D, 1 + freed))
                        if kind == "proj":
                            oc, half = divmod(a, 2)
                            if a == 2:
                                pe.wait_ge(o_copied, count(6, 1 + 6))
                            if a == 3:
                                pe.wait_ge(den_copied, count(6, 1 + 6))
                            pe.wait_ge(ao_done, count(6, 1 + 6))
                            for k in range(KC):
                                last = mm(out, wproj[:, k, oc * P:oc * P + P], ao[:, k, half * 512:half * 512 + 512],
                                          start=(k == 0), stop=(k == KC - 1))
                        elif kind == "vp":
                            last = value_tile(a, out)
                        elif kind == "gs1":
                            pe.wait_ge(mv_ready, count(2, 3))
                            last = group_stats(out)
                        elif kind == "gs2":
                            pe.wait_ge(gb_ready, count(2, 3))
                            last = group_back(out)
                        elif kind in ("cen", "vc"):
                            pe.wait_ge(pxn_ready, count(1, 1))
                            w = wf if kind == "cen" else wv
                            for k in range(KC):
                                last = mm(out[0:64, 0:C], pxn[:, k, :], w[:, k, :], start=(k == 0), stop=(k == KC - 1))
                        elif kind in ("f", "v"):
                            q, hf = divmod(a, 2)
                            if kind == "f" and a in (0, 4):
                                pe.wait_ge(xn1_ready, count(2, 1 + a // 4))
                            w = wf if kind == "f" else wv
                            for k in range(KC):
                                last = mm(out[:, 0:C], xn1[:, k, q, hf * P:hf * P + P], w[:, k, :],
                                          start=(k == 0), stop=(kind == "v" and k == KC - 1))
                            if kind == "f":
                                last = mm(out[:, 0:C], ones[0:1, :], bfb[0:1, :], start=False, stop=True)
                        elif kind == "cenT":
                            pe.wait_ge(cen_ready, count(1, 1))
                            for k in range(KC):
                                last = mm(out[:, 64 * k:64 * k + 64], cen[:, k * P:k * P + P], ident[0:64, 0:64],
                                          start=True, stop=True)
                        elif kind == "gc":
                            pe.wait_ge(bd_ready, count(1, 1))
                            for k in range(KC):
                                last = mm(out[96:97, :], bf_c[:, k:k + 1], bdc[:, k, :], start=(k == 0), stop=(k == KC - 1))
                        elif kind == "G":
                            for k in range(KC):
                                last = mm(out, wfn[:, k, a * P:a * P + P], bdc[:, k, :], start=(k == 0), stop=(k == KC - 1))
                        elif kind == "num":
                            if a == 0:
                                pe.wait_ge(l_act, count(L1_A, 1 + act_items("G", 2)))
                                pe.wait_ge(l_dve, count(L1_D, 1 + sum(w == "D" for _, _, _, w in L1[:L1_AT["gc", 0] + 1])))
                            for hf in range(2):
                                o = out[:, hf * P:hf * P + P]
                                for k in range(KC):
                                    mm(o, xn1[:, k, a, hf * P:hf * P + P], gmat[:, k, a * P:a * P + P],
                                       start=(k == 0), stop=False)
                                last = mm(o, ones[96:97, :], gcr[:, a * P:a * P + P], start=False, stop=True)
                        elif kind == "agg":
                            pe.wait_ge(sim_ready, count(QUADS, a + 1))
                            for hf in range(2):
                                mm(out[:, 0:VW], simm[:, a % 2, hf * P:hf * P + P], vt1[:, 2 * a + hf, :],
                                   start=(hf == 0), stop=False)
                            last = mm(out[:, 0:VW], sel_q[:, a, :], vcx[:, :], start=False, stop=True)
                        elif kind == "sT":
                            for hf in range(2):
                                last = nc.tensor.transpose(out[:, hf * P:hf * P + P], simm[:, a % 2, hf * P:hf * P + P], ident)
                        elif kind == "aT":
                            pe.wait_ge(agg_ready, count(QUADS, a + 1))
                            for k in range(KC):
                                last = nc.tensor.transpose(out[:, k * P:k * P + P], agg[:, k * P:k * P + P], ident)
                        elif kind == "MT":
                            pe.wait_ge(l_act, count(L1_A, 1 + act_items("aT", a)))
                            for k in range(KC):
                                last = mm(out[:, 0:C], aggt[:, k, :], wp[:, k, :], start=(k == 0), stop=(k == KC - 1))
                        elif kind in ("outa", "outb"):
                            pe.wait_ge(l_act, count(L1_A, 1 + act_items("MT", a)))
                            for e, oc in enumerate((0, 1) if kind == "outa" else (2,)):
                                last = mm(out[:, e * QT:e * QT + QT], mts[:, oc * P:oc * P + P], simt, start=True, stop=True)
                        last.then_inc(l_ready, 1)
                        for kind, a in LATE_WORK.get((kind, a), ()):
                            fill(3 if kind == "nm" else 2, kind, a)

        @block.scalar
        def _(act):
            def norm0(slot, k):
                return nc.scalar.activation(xn[:, k, :], xs[:, slot, k, :], ACT.Identity,
                                            bias=sc0[:, k, 1:2], scale=sc0[:, k, 0:1])

            act.sem_inc(exp_done, 2)
            act.sem_inc(o_copied, 1)
            act.sem_inc(den_copied, 1)
            act.sem_inc(l_act, 1)
            act.wait_ge(sc_ready, 1)
            for k in range(KC):
                norm0(0, k).then_inc(xn_ready, 1)
            for i, (kind, a) in enumerate(PRE_WORK):
                if kind in ("qk", "qk1"):
                    if kind == "qk1" and a == 0:
                        for h in range(HPG):
                            act.wait_ge(stack_in[h], 96)
                    act.wait_ge(work_ready, i + 1)
                    nc.scalar.activation(qkn[:, a // 4, 0, (a % 4) * 256:(a % 4) * 256 + 256], work[i % 2][:, 0:256],
                                         ACT.Copy).then_inc(qk_hi, 1)

            with act.Fori(0, PAIRS) as it:
                for j in range(2):
                    def count(per, n):
                        return it * (2 * per) + (j * per + n)
                    done = 0

                    def copy_denominators(H):
                        act.wait_ge(den_done, count(24, 1 + 4 * H + 4))
                        act.wait_ge(ao_done, count(6, 1 + H))
                        nc.scalar.activation(rden[:, :], dbank, ACT.Copy).then_inc(den_copied, 1)

                    for S in range(GROUPS * STEPS + 1):
                        g, s = divmod(S, STEPS)
                        if S < GROUPS * STEPS:
                            for p in range(2):
                                t = 2 * S + p
                                act.wait_ge(score_ready, count(96, t + 1))
                                act.wait_ge(pv_done, count(48, S + 1))
                                act.wait_ge(sum_done, count(48, 2 * ((S - 3) // 2) + p + 5))
                                nc.scalar.activation(prob[:, t % 6, :], score[p][:, :, :].rearrange("p e n -> p (e n)"),
                                                     ACT.Exp, scale=SCALE0).then_inc(exp_done, 1)
                                if p == 0 and S % 8 == 1 and S > 8:
                                    H = S // 8 - 1
                                    act.wait_ge(pv_done, count(48, 3 + 8 * (H + 1)))
                                    nc.scalar.activation(ao[:, H // 2, (H % 2) * 512:(H % 2) * 512 + 512], obank,
                                                         ACT.Copy).then_inc(o_copied, 1)
                                if p == 0 and S % 8 == 2 and S > 8:
                                    copy_denominators(S // 8 - 1)
                        else:
                            act.wait_ge(pv_done, count(48, 3 + 48))
                            nc.scalar.activation(ao[:, 2, 512:1024], obank, ACT.Copy).then_inc(o_copied, 1)
                            copy_denominators(5)
                        for kind, a in WORK[S]:
                            if kind == "qk":
                                if a == 0:
                                    for h in range(HPG):
                                        act.wait_ge(stack_in[h], count(3 * 96, 96 * (g + 2)))
                                act.wait_ge(work_ready, count(WORK_N, PRE_N + done + 1))
                                nc.scalar.activation(qkn[:, a // 4, 0, (a % 4) * 256:(a % 4) * 256 + 256],
                                                     work[done % 2][:, 0:256], ACT.Copy).then_inc(qk_hi, 1)
                                if g == 0 and a == 7:
                                    qk_end = done
                            done += 1
                        if S in (17, 18, 19):
                            if S == 17:
                                act.wait_ge(sc_ready, count(2, 2))
                                act.wait_ge(work_ready, count(WORK_N, PRE_N + qk_end + 1))
                            norm0(1 - j, S - 17).then_inc(xn_ready, 1)

                    def item(kind, a):
                        n = L1_AT[kind, a]
                        act.wait_ge(l_ready, count(L1_N, n + 1))
                        return lb[L1[n][2]]

                    def value_copy(a):
                        nc.scalar.activation(vt0[:, a, :], item("vp", a)[:, 0:C], ACT.Copy).then_inc(l_act, 1)
                    for a in range(7):
                        value_copy(a)
                    act.wait_ge(sc_ready, count(2, 3))
                    for f1 in range(2):
                        for k in range(KC):
                            src = xs[:, j, k, 512 * f1:512 * f1 + 512].rearrange("p (y f x) -> p f y x", y=16, f=2)
                            dst = xn1[:, k, 2 * f1:2 * f1 + 2, :].rearrange("p f (y x) -> p f y x", y=16)
                            last = nc.scalar.activation(dst, src, ACT.Identity, bias=sc1[:, k, 1:2], scale=sc1[:, k, 0:1])
                        last.then_inc(xn1_ready, 1)
                    value_copy(7)
                    nc.scalar.activation(vcx[:, 0:C], item("vc", 0)[0:64, 0:C], ACT.Copy).then_inc(l_act, 1)
                    for t in range(8):
                        out = item("f", t)
                        act.wait_ge(sq_used, count(8, t + 1))
                        nc.scalar.activation(sq[:, t % 2, :], out[:, 0:C], ACT.Square).then_inc(l_act, 1)
                        if t in (5, 6, 7):
                            nc.scalar.activation(gmat[:, t - 5, :], item("G", t - 5), ACT.Copy).then_inc(l_act, 1)

                    def sim_exp(q):
                        act.wait_ge(cos_ready, count(QUADS, q + 1))
                        nc.scalar.activation(cosb, cosb, ACT.Exp, bias=nbeta, scale=nalpha).then_inc(sexp_ready, 1)

                    def sim_t(q):
                        nc.scalar.activation(simt, item("sT", q)[:, 0:QT], ACT.Copy).then_inc(l_act, 1)
                    sim_exp(0)
                    sim_exp(1)
                    sim_t(0)
                    for q in range(QUADS):
                        nc.scalar.activation(aggt.rearrange("p k n -> p (k n)"), item("aT", q)[:, 0:C], ACT.Copy).then_inc(l_act, 1)
                        if q + 2 < QUADS:
                            sim_exp(q + 2)
                        nc.scalar.activation(mts, item("MT", q)[:, 0:C], ACT.Copy).then_inc(l_act, 1)
                        if q + 1 < QUADS:
                            sim_t(q + 1)

        @block.vector
        def _(dve):
            v = nc.vector
            linked = [0]
            base = [0]

            def link(ins):
                linked[0] += 1
                ins.then_inc(chain, 1)
                dve.wait_ge(chain, base[0] + linked[0])

            def channel_stats(slot, k, half):
                v.bn_stats(st6[:, k, half, :], xs[:, slot, k, half * 512:half * 512 + 512])

            def channel_moments():
                for k in range(KC):
                    last = v.bn_aggr(mv[:, k, :], st6[:, k, :, :])
                link(last)
                link(v.tensor_tensor(mxs[:, 0:KC], mv[:, :, 0], mv[:, :, 0], ALU.mult))
                v.tensor_tensor(mv[:, :, 1], mv[:, :, 1], mxs[:, 0:KC], ALU.add).then_inc(mv_ready, 1)

            G = slice(64, 96)
            g_scale, g_shift, g_mean, g_sq, g_var = (gst[G, i:i + 1] for i in range(5))

            def group_variance():
                link(v.scalar_tensor_tensor(out=g_var, in0=g_mean, scalar=g_mean, in1=g_sq, op0=ALU.mult, op1=ALU.subtract))
                v.tensor_scalar(g_var, g_var, -1.0, GN_EPS, ALU.mult, ALU.add).then_inc(var_ready, 1)

            def group_shift():
                v.scalar_tensor_tensor(out=g_shift, in0=g_mean, scalar=-1.0, in1=g_scale,
                                       op0=ALU.mult, op1=ALU.mult).then_inc(gb_ready, 1)

            def max_item(m, out):
                i = m // 2 % 16
                v.tensor_reduce(mx[:, m // 32, i, m % 2:m % 2 + 1], out, AX.X, ALU.max).then_inc(work_free, 1)

            def negated_maxima(half):
                v.tensor_reduce(nmx[:, :], mx[:, half, :, :], AX.X, ALU.max, negate=True).then_inc(negmax, 1)

            def maxima_parts(out):
                link(v.tensor_copy(nmp[:, 0, :], out[0:16, 0:P]))
                v.tensor_tensor(nmp[:, 1, :], out[0:16, 0:P], nmp[:, 0, :].bitcast(f32), ALU.subtract).then_inc(nm_ready, 1)

            def low_part(a, out):
                r = slice((a % 4) * 256, (a % 4) * 256 + 256)
                v.tensor_tensor(qkn[:, a // 4, 1, r], out[:, 0:256], qkn[:, a // 4, 0, r].bitcast(f32), ALU.subtract).then_inc(qk_lo, 1)

            dve.sem_inc(work_free, 2)
            dve.sem_inc(sq_used, 2)
            dve.sem_inc(ao_done, 1)
            dve.sem_inc(l_dve, 1)
            for b in range(2):
                v.memset(ks[96:98, b, :, :].bitcast(f32), 1.0)
            dve.wait_ge(const_in, 16 * 20)
            link(v.tensor_scalar(cols[:, 9:11], cols[:, 9:11], -1.0, None, ALU.mult))
            v.tensor_tensor(bvm[:, :], bvm[:, :], mask_hm, ALU.mult).then_inc(const_done, 1)

            dve.wait_ge(x_in, 16 * KC)
            for k in range(KC):
                for half in range(2):
                    last = v.bn_stats(st6[:, k, half, :], xs[:, 0, k, half * 512:half * 512 + 512])
            link(last)
            channel_moments()
            for i, (kind, a) in enumerate(PRE_WORK):
                out = work[i % 2]
                if kind == "max":
                    dve.wait_ge(work_ready, i + 1)
                    max_item(a, out)
                    if a in (31, 63):
                        dve.wait_ge(work_free, 2 + i + 1)
                        negated_maxima(a // 32)
                elif kind == "nm":
                    dve.wait_ge(work_ready, i + 1)
                    dve.wait_ge(nm_in, 32 * a)
                    maxima_parts(out)
                    dve.wait_ge(nm_ready, a + 1)
                    dve.sem_inc(work_free, 1)
                elif kind in ("qk", "qk1"):
                    dve.wait_ge(qk_hi, (8 if kind == "qk1" else 0) + a + 1)
                    low_part(a, out)
                    dve.wait_ge(qk_lo, (8 if kind == "qk1" else 0) + a + 1)
                    dve.sem_inc(work_free, 1)
                elif kind == "v":
                    dve.wait_ge(work_ready, i + 1)
                    link(v.tensor_copy(vt0[:, a, :], out[:, 0:C]))
                    dve.sem_inc(work_free, 1)
                    dve.sem_inc(v0_ready, 1)
                elif kind == "gs1":
                    dve.wait_ge(work_ready, i + 1)
                    link(v.tensor_copy(gst[G, 2:4], out[G, 0:2]))
                    dve.sem_inc(work_free, 1)
                    group_variance()
                    dve.wait_ge(rstd_ready, 1)
                    group_shift()
                else:
                    dve.wait_ge(work_ready, i + 1)
                    link(v.tensor_copy(sc0[:, :, :].rearrange("p k n -> p (k n)"), out[:, 0:6]))
                    dve.sem_inc(work_free, 1)
                    dve.sem_inc(sc_ready, 1)
            pre_links = linked[0]

            with dve.Fori(0, PAIRS) as it:
                base[0] = it * CHAIN_PAIR
                for j in range(2):
                    def count(per, n):
                        return it * (2 * per) + (j * per + n)
                    done = 0

                    def released(ins):
                        ins.then_inc(work_free, 1)
                        dve.wait_ge(work_free, count(WORK_N, PRE_N + 2 + done + 1))

                    def use(g, kind, a):
                        nonlocal done
                        out = work[done % 2]
                        if kind != "qk":
                            dve.wait_ge(work_ready, count(WORK_N, PRE_N + done + 1))
                        if kind == "max":
                            max_item(a, out)
                            if a in (31, 63):
                                dve.wait_ge(work_free, count(WORK_N, PRE_N + 2 + done + 1))
                                negated_maxima(a // 32)
                        elif kind == "nm":
                            n = 2 * g + 3 if a == 0 else 2 * g + 2
                            dve.wait_ge(nm_in, count(6 * 32, 32 * (n - 1)))
                            maxima_parts(out)
                            dve.wait_ge(nm_ready, count(6, n))
                            dve.sem_inc(work_free, 1)
                        elif kind == "qk":
                            dve.wait_ge(qk_hi, count(24, 16 + 8 * g + a + 1))
                            low_part(a, out)
                            dve.wait_ge(qk_lo, count(24, 16 + 8 * g + a + 1))
                            dve.sem_inc(work_free, 1)
                        elif kind == "gs1":
                            released(v.tensor_copy(gst[G, 2:4], out[G, 0:2]))
                            group_variance()
                        else:
                            released(v.tensor_copy(sc0[:, :, :].rearrange("p k n -> p (k n)"), out[:, 0:6]))
                            dve.sem_inc(sc_ready, 1)
                        done += 1

                    def late(kind, a=0):
                        for what, m in LATE_WORK.get((kind, a), ()):
                            use(3 if what == "nm" else 2, what, m)

                    def denominators_part(H, i):
                        if i == 0:
                            dve.wait_ge(den_copied, count(6, 1 + H + 1))
                        r = rden[:, i * P:i * P + P]
                        ins = v.reciprocal(r, r)
                        if i == 3:
                            link(ins)
                            o = ao[:, H // 2, (H % 2) * 512:(H % 2) * 512 + 512]
                            v.tensor_tensor(o, o, rden[:, :], ALU.mult).then_inc(ao_done, 1)

                    for S in range(GROUPS * STEPS + 1):
                        g = S // STEPS
                        if S == 0:
                            dve.wait_ge(x_in, count(16 * KC, 32 * KC))
                        if S < 6:
                            last = v.bn_stats(st6[:, S // 2, S % 2, :], xs[:, 1 - j, S // 2, (S % 2) * 512:(S % 2) * 512 + 512])
                            if S == 5:
                                link(last)
                        if S == 11:
                            dve.wait_ge(rstd_ready, count(2, 2))
                            group_shift()
                        for kind, a in WORK[S]:
                            use(g, kind, a)
                        if S == 5:
                            channel_moments()
                        if S > 10 and 3 <= S % 8 <= 6:
                            denominators_part(S // 8 - 1, S % 8 - 3)
                    for i in range(4):
                        late("vp", i)
                        denominators_part(5, i)
                    late("vp", 4)

                    freed = [0]

                    def item(kind, a=0):
                        n = L1_AT[kind, a]
                        assert sum(w == "D" for _, _, _, w in L1[:n]) == freed[0], (kind, a)
                        dve.wait_ge(l_ready, count(L1_N, n + 1))
                        return lb[L1[n][2]]

                    def read(ins, then=False):
                        freed[0] += 1
                        ins.then_inc(l_dve, 1)
                        if then:
                            dve.wait_ge(l_dve, count(L1_D, 1 + freed[0]))

                    for i in range(6):
                        oc, half = divmod(i, 2)
                        o = xs[:, j, oc, half * 512:half * 512 + 512]
                        read(v.scalar_tensor_tensor(out=o, in0=item("proj", i), scalar=pb_c[:, oc:oc + 1], in1=o,
                                                    op0=ALU.add, op1=ALU.add), then=True)
                        last = v.bn_stats(st6[:, oc, half, :], o)
                        if i < 5:
                            late("proj", i)
                    link(last)
                    for k in range(KC):
                        last = v.tensor_reduce(pool1[:, k, :], xs[:, j, k, :].rearrange("p (n i) -> p n i", i=4), AX.X, ALU.add)
                    link(last)
                    for k in range(KC):
                        for f1 in range(2):
                            src = pool1[:, k, 128 * f1:128 * f1 + 128].rearrange("p (w i f h) -> p f w h i", w=4, i=4, f=2)
                            dst = pxn[:, k, 32 * f1:32 * f1 + 32].rearrange("p (f w h) -> p f w h", f=2, w=4)
                            last = v.tensor_reduce(dst, src, AX.X, ALU.add)
                    link(last)
                    v.tensor_scalar(pxn[:, :, :], pxn[:, :, :], 1.0 / 16, None, ALU.mult)
                    channel_moments()
                    late("proj", 5)
                    read(v.tensor_copy(gst[G, 2:4], item("gs1")[G, 0:2]), then=True)
                    group_variance()
                    late("gs1")
                    dve.wait_ge(rstd_ready, count(2, 3))
                    group_shift()
                    late("vp", 6)
                    read(v.tensor_copy(sc1[:, :, :].rearrange("p k n -> p (k n)"), item("gs2")[:, 0:6]), then=True)
                    dve.sem_inc(sc_ready, 1)
                    for k in range(KC):
                        last = v.tensor_scalar(pxn[:, k, :], pxn[:, k, :], sc1[:, k, 0:1], sc1[:, k, 1:2], ALU.mult, ALU.add)
                    last.then_inc(pxn_ready, 1)
                    late("gs2")
                    v.memset(vt1[:, :, C:VW], 1.0)
                    v.memset(vcx[:, C:VW], 1.0)
                    read(v.tensor_tensor(cen, item("cen")[0:64, 0:C], bfb[:, :], ALU.add), then=True)
                    link(v.tensor_tensor(csq, cen, cen, ALU.mult))
                    link(v.tensor_reduce(cn2[:, 0, :], csq.rearrange("p (h d) -> p h d", h=HEADS1), AX.X, ALU.add))
                    v.tensor_scalar(cn2[:, 0, :], cn2[:, 0, :], NORM_EPS2, None, ALU.max).then_inc(cnorm_ready, 1)

                    def tile_values(t):
                        read(v.tensor_copy(vt1[:, t, 0:C], item("v", t)[:, 0:C]))

                    def tile_norms(t):
                        dve.wait_ge(l_act, count(L1_A, 1 + act_items("f", t)))
                        v.tensor_reduce(nsq[:, t, :], sq[:, t % 2, :].rearrange("p (h d) -> p h d", h=HEADS1),
                                        AX.X, ALU.add).then_inc(sq_used, 1)

                    late("vc")
                    tile_values(0)
                    dve.wait_ge(crn_ready, count(1, 1))
                    v.tensor_tensor(cen.rearrange("p (h d) -> p h d", h=HEADS1), cen.rearrange("p (h d) -> p h d", h=HEADS1),
                                    cn2[:, 1, :].unsqueeze(2).to_broadcast((64, HEADS1, DH1)), ALU.mult).then_inc(cen_ready, 1)
                    tile_norms(0)
                    for t in range(1, 8):
                        if t == 1:
                            late("f", 1)
                        tile_values(t)
                        tile_norms(t)
                        if t == 2:
                            out = item("cenT")
                            for k in range(KC):
                                ins = v.tensor_tensor(
                                    bdc[:, k, :].rearrange("p (q h m) -> p q h m", q=QUADS, h=HEADS1),
                                    out[:, 64 * k:64 * k + 64].rearrange("p (q m) -> p q m", q=QUADS).unsqueeze(2)
                                       .to_broadcast((P, QUADS, HEADS1, CENT)),
                                    mask_d[:, k, :].unsqueeze(1).unsqueeze(3).to_broadcast((P, QUADS, HEADS1, CENT)), ALU.mult)
                            read(ins, then=True)
                            dve.sem_inc(bd_ready, 1)
                        if t % 2:
                            dve.wait_ge(sq_used, count(8, 2 + t + 1))
                            v.tensor_scalar(nsq[:, t - 1:t + 1, :], nsq[:, t - 1:t + 1, :], NORM_EPS2, None,
                                            ALU.max).then_inc(norm_ready, 1)
                        if t == 4:
                            read(v.tensor_copy(gcr, item("gc")[96:97, :]))

                    def hmview(ap):
                        return ap.rearrange("p (t m) -> p t m", m=CENT)

                    def over_centres(ap):
                        return ap.unsqueeze(2).to_broadcast((P, 2 * HEADS1, CENT))

                    def cosines(q):
                        dve.wait_ge(rn_ready, count(QUADS, q + 1))
                        read(v.tensor_tensor(hmview(cosb), hmview(item("num", q)[:, 0:QT]),
                                             over_centres(rn[:, 2 * q:2 * q + 2, :].rearrange("p t h -> p (t h)")), ALU.mult), then=True)
                        dve.sem_inc(cos_ready, 1)

                    def sigmoids(q):
                        dve.wait_ge(sexp_ready, count(QUADS, q + 1))
                        link(v.tensor_scalar(cosb, cosb, 1.0, None, ALU.add))
                        link(v.reciprocal(sig, cosb))

                    def only_first_largest(q):
                        link(v.tensor_reduce(mxs[:, :], hmview(sig), AX.X, ALU.max))
                        link(v.tensor_tensor(hmview(eq), hmview(sig), over_centres(mxs[:, :]), ALU.is_equal))
                        link(v.tensor_tensor(hmview(wgt), hmview(eq),
                                             first_w.unsqueeze(1).to_broadcast((P, 2 * HEADS1, CENT)), ALU.mult))
                        link(v.tensor_reduce(mw[:, :], hmview(wgt), AX.X, ALU.max))
                        link(v.tensor_tensor(hmview(eq), hmview(wgt), over_centres(mw[:, :]), ALU.is_equal))
                        if q >= 2:
                            dve.wait_ge(l_ready, count(L1_N, L1_AT["sT", q - 2] + 1))
                        v.tensor_tensor(simm[:, q % 2, :], eq, sig, ALU.mult).then_inc(sim_ready, 1)

                    def aggregates(q):
                        out = item("agg", q)
                        link(v.reciprocal(rs[:, :], out[:, C:VW]))
                        read(v.scalar_tensor_tensor(out=agg, in0=out[:, 0:C], scalar=rs[:, :], in1=mask_hm,
                                                    op0=ALU.mult, op1=ALU.mult), then=True)
                        v.tensor_tensor(agg, agg, bvm[:, :], ALU.add).then_inc(agg_ready, 1)

                    def outputs(q):
                        for kind, ocs in (("outa", (0, 1)), ("outb", (2,))):
                            out = item(kind, q)
                            for e, oc in enumerate(ocs):
                                o = quad_view(xs[:, j, oc, :], q)
                                ins = v.scalar_tensor_tensor(out=o, in0=out[:, e * QT:e * QT + QT].rearrange("p (y x) -> p y x", y=16),
                                                             scalar=bp_c[:, oc:oc + 1], in1=o, op0=ALU.add, op1=ALU.add)
                            read(ins, then=(kind == "outb"))
                        dve.sem_inc(y_ready, 1)

                    cosines(0)
                    sigmoids(0)
                    cosines(1)
                    only_first_largest(0)
                    aggregates(0)
                    for q in range(QUADS):
                        if q + 1 < QUADS:
                            sigmoids(q + 1)
                            if q + 2 < QUADS:
                                cosines(q + 2)
                            only_first_largest(q + 1)
                            aggregates(q + 1)
                        outputs(q)
                assert linked[0] == pre_links + CHAIN_PAIR, (linked[0], pre_links)

        @block.gpsimd
        def _(pool):
            pool.sem_inc(sum_done, 4)
            pool.wait_ge(const_in, 16 * 20)
            pool.wait_ge(var_ready, 1)
            nc.gpsimd.tensor_tensor(gst[64:96, 0:1], gst[64:96, 4:5], neg_half[64:96, :], ALU.pow).then_inc(rstd_ready, 1)
            with pool.Fori(0, PAIRS) as it:
                for j in range(2):
                    def count(per, n):
                        return it * (2 * per) + (j * per + n)
                    for d in range(24):
                        for p in range(2):
                            pool.wait_ge(exp_done, count(96, 2 + 4 * d + 2 + p + 1))
                            pool.wait_ge(den_done, count(24, 1 + d))
                            nc.gpsimd.tensor_tensor(psums[:, p, :], prob[:, (4 * d + p) % 6, :],
                                                    prob[:, (4 * d + 2 + p) % 6, :], ALU.add).then_inc(sum_done, 1)
                        if d == 4:
                            pool.wait_ge(var_ready, count(2, 2))
                            pool.wait_ge(sum_done, count(48, 2 * d + 6))
                            nc.gpsimd.tensor_tensor(gst[64:96, 0:1], gst[64:96, 4:5], neg_half[64:96, :],
                                                    ALU.pow).then_inc(rstd_ready, 1)
                            pool.wait_ge(rstd_ready, count(2, 2))
                    pool.wait_ge(var_ready, count(2, 3))
                    pool.wait_ge(sum_done, count(48, 52))
                    nc.gpsimd.tensor_tensor(gst[64:96, 0:1], gst[64:96, 4:5], neg_half[64:96, :],
                                            ALU.pow).then_inc(rstd_ready, 1)
                    pool.wait_ge(rstd_ready, count(2, 3))
                    pool.wait_ge(cnorm_ready, count(1, 1))
                    nc.gpsimd.tensor_tensor(cn2[:, 1, :], cn2[:, 0, :], neg_half[0:64, :].to_broadcast((64, HEADS1)),
                                            ALU.pow).then_inc(crn_ready, 1)
                    for q in range(QUADS):
                        pool.wait_ge(norm_ready, count(QUADS, q + 1))
                        nc.gpsimd.tensor_tensor(rn[:, 2 * q:2 * q + 2, :].rearrange("p t h -> p (t h)"),
                                                nsq[:, 2 * q:2 * q + 2, :].rearrange("p t h -> p (t h)"),
                                                neg_half.to_broadcast((P, 2 * HEADS1)), ALU.pow).then_inc(rn_ready, 1)


CHAIN_PAIR = 112
SAMPLES = 16


def constants():
    import numpy as np
    c = np.zeros((P, C_COLS), np.float32)
    c[:, C_ID:C_ID + P] = np.eye(P)
    ch = np.arange(C)
    size = C // GN_GROUPS
    for k in range(KC):
        for p in range(P):
            c[p, C_GA + k * 32 + (k * P + p) // size] = 1.0 / size
            c[p, C_MD + k * HEADS1 + (k * P + p) // DH1] = 1.0
    hm = np.arange(P)
    c[:, C_BD:C_BD + C] = hm[:, None] // CENT == ch[None, :] // DH1
    for q in range(QUADS):
        for m in range(CENT):
            c[q * CENT + m, C_SEL + q * P + m:C_SEL + (q + 1) * P:CENT] = 1.0
    c[64:96, C_SEL:C_SEL + C] = ch[None, :] // size == np.arange(GN_GROUPS)[:, None]
    c[:, C_W16:C_W16 + CENT] = CENT - np.arange(CENT)
    c[:, C_ONE:C_ONE + P] = 1.0
    c[:, C_NH] = -0.5
    return c


def kernel(x, L0_conv_qkv_w, L0_conv_proj_w, L0_conv_proj_b, L1_conv_Wf, L1_conv_bf, L1_conv_Wv, L1_conv_bv,
           L1_conv_Wp, L1_conv_bp, L1_conv_sim_alpha, L1_conv_sim_beta):
    import concourse.bacc as bacc
    import numpy as np
    from concourse.bass_utils import run_bass_kernel_spmd

    x = np.asarray(x)
    samples = x.shape[0]
    tokens = x.reshape(samples, C, N)
    a = np.ascontiguousarray
    arrays = {
        "x": np.concatenate([tokens, tokens[:2]]),
        "qkv_t": a(np.asarray(L0_conv_qkv_w).T), "proj_t": a(np.asarray(L0_conv_proj_w).T),
        "proj_b": np.asarray(L0_conv_proj_b), "wf_t": a(np.asarray(L1_conv_Wf).T), "wf_n": np.asarray(L1_conv_Wf),
        "bf": np.asarray(L1_conv_bf), "wv_t": a(np.asarray(L1_conv_Wv).T), "bv": np.asarray(L1_conv_bv),
        "wp_t": a(np.asarray(L1_conv_Wp).T), "bp": np.asarray(L1_conv_bp),
        "alpha": np.asarray(L1_conv_sim_alpha), "beta": np.asarray(L1_conv_sim_beta), "consts": constants(),
    }
    nc = bacc.Bacc("TRN2", target_bir_lowering=False, num_devices=1, dynamic_dma_scratch_size=1024)
    args = [nc.dram_tensor(n, v.shape, mybir.dt.float32, kind="ExternalInput").ap() for n, v in arrays.items()]
    y = nc.dram_tensor("y", (samples, C, N), mybir.dt.float32, kind="ExternalOutput").ap()
    conv_kernel(nc, samples, *args, y)
    got = run_bass_kernel_spmd(nc, [arrays], core_ids=[0])
    return got.results[0]["y"].reshape(samples, C, 32, 32)
```

```python
from contextlib import ExitStack

import concourse.bass as bass
from concourse import mybir

P = 128
C, KC = 384, 3
N = 1024
HEADS0, DH0 = 12, 32
GROUPS, HPG = 3, 4
HEADS1, DH1 = 8, 48
QUADS, QT = 4, 256
CENT = 16
HM = HEADS1 * CENT
STEPS = 16
SCALE0 = float(DH0) ** -0.5
GN_GROUPS, GN_EPS = 32, 1e-5
NORM_EPS2 = 1e-24
VW = C + 1
KROWS = 98

C_ID, C_GA, C_BD, C_MD, C_SEL, C_W16, C_ONE, C_NH = 0, 128, 224, 608, 632, 1144, 1160, 1288
C_COLS = 1289



QK_STEPS = (5, 7, 8, 10, 11, 13, 14, 15)


def work_items():
    at = [[] for _ in range(GROUPS * STEPS + 1)]
    spread = [0, 0, 4, 5, 5, 5, 5, 4, 5, 6, 4, 4, 6, 4, 4, 3]
    last = [0, 0, 2, 3, 2, 3, 2, 3, 2, 3, 2, 3, 2, 3, 2, 0]
    for g in range(GROUPS):
        m = 0
        for s in range(STEPS):
            n = (last if g == GROUPS - 1 else spread)[s]
            at[g * STEPS + s] += [("max", m + i) for i in range(n)]
            m += n
            if s == (15 if g == GROUPS - 1 else 10):
                at[g * STEPS + s].append(("nm", 0))
            if s in QK_STEPS:
                at[g * STEPS + s].append(("qk", QK_STEPS.index(s)))
        assert m == (32 if g == GROUPS - 1 else 64)
        if g < GROUPS - 1:
            at[(g + 1) * STEPS + 1].append(("nm", 1))
    at[11].append(("gs1", 0))
    at[15].append(("gs2", 0))
    return at


WORK = work_items()
LATE_WORK, tile = {}, 32
for after, n in ((("vp", 0), 2), (("vp", 1), 2), (("vp", 2), 2), (("proj", 0), 1), (("proj", 1), 1), (("proj", 2), 1),
                 (("proj", 3), 1), (("proj", 4), 1), (("proj", 5), 1), (("gs1", 0), 2), (("gs2", 0), 2), (("f", 0), 2),
                 (("v", 0), 2), (("vc", 0), 2), (("f", 1), 2), (("v", 1), 2), (("f", 2), 2), (("v", 2), 2), (("f", 3), 2)):
    LATE_WORK[after] = [("max", tile + i) for i in range(n)]
    tile += n
assert tile == 64
LATE_WORK["f", 5] = [("nm", 1)]
WORK_N = sum(map(len, WORK)) + sum(map(len, LATE_WORK.values()))
PRE_WORK = ([("gs1", 0), ("gs2", 0)] + [("qk", c) for c in range(8)] + [("v", t) for t in range(8)]
            + [("max", m) for m in range(32)] + [("nm", 0)] + [("max", m) for m in range(32, 64)]
            + [("nm", 1)] + [("qk1", c) for c in range(8)])
PRE_N = len(PRE_WORK)
assert WORK_N % 2 == 0 and PRE_N % 2 == 0


def layer1_items():
    out = [("vp", i, 2 + i % 2, "A") for i in range(5)]
    out += [("proj", i, (0, 1, 6, 7, 0, 1)[i], "D") for i in range(6)]
    out += [("gs1", 0, 6, "D"), ("vp", 5, 3, "A"), ("vp", 6, 2, "A"), ("gs2", 0, 7, "D"), ("vp", 7, 3, "A")]
    order = ("f0 v0 cen0/2D vc0/3A f1 v1 cenT0/2D f2 v2 gc0/3D G0/2A f3 v3 G1/3A G2/2A num0/3D f4 v4 f5 agg0/2D sT0/3A num1/2D v5 "
             "aT0/3A f6 v6 MT0/2A agg1/3D outa0/1D outb0/7D num2/2D f7 v7 sT1/3A aT1/1A MT1/2A agg2/3D outa1/7D "
             "outb1/0D num3/1D sT2/6A aT2/2A MT2/3A agg3/7D outa2/0D outb2/1D sT3/6A aT3/2A MT3/3A outa3/7D outb3/0D")
    for name in order.split():
        name, _, place = name.partition("/")
        kind, i = name[:-1], int(name[-1])
        if kind == "f":
            out += [(kind, i, i % 2, "A")]
        elif kind == "v":
            out += [(kind, i, 6 + i % 2, "D")]
        else:
            out += [(kind, i, int(place[0]), place[1])]
    return out


L1 = layer1_items()
L1_AT = {(k, i): n for n, (k, i, _, _) in enumerate(L1)}
L1_N = len(L1)
L1_D = sum(w == "D" for _, _, _, w in L1)
L1_A = L1_N - L1_D


def freed_before(n):
    bank = L1[n][2]
    for m in range(n - 1, -1, -1):
        if L1[m][2] == bank:
            who = L1[m][3]
            return who, sum(w == who for _, _, _, w in L1[:m + 1])
    return None, 0


def sums(step, pair):
    quad, i = divmod(step, 4)
    return 6 * quad + 2 * (max(i, 1) - 1) + pair + 1


def act_items(kind, i):
    return sum(w == "A" for _, _, _, w in L1[:L1_AT[kind, i] + 1])


def conv_kernel(nc, samples, x, qkv_t, proj_t, proj_b, wf_t, wf_n, bf, wv_t, bv, wp_t, bp, alpha, beta, consts, y):
    f32, f32r = mybir.dt.float32, mybir.dt.float32r
    ALU, ACT, AX = mybir.AluOpType, mybir.ActivationFunctionType, mybir.AxisListType
    ctx = ExitStack()
    with ctx:
        def sb(name, shape, dt=f32):
            return ctx.enter_context(nc.sbuf_tensor(name, shape, dt))

        def sem(name):
            return ctx.enter_context(nc.semaphore(name))

        cst = sb("cst", [P, C_COLS])
        ident = cst[:, C_ID:C_ID + P]
        grp_avg = cst[:, C_GA:C_GA + 96].rearrange("p (k g) -> p k g", k=KC)
        mask_hm = cst[:, C_BD:C_BD + C]
        mask_d = cst[:, C_MD:C_MD + 24].rearrange("p (k h) -> p k h", k=KC)
        sel_q = cst[0:64, C_SEL:C_SEL + 512].rearrange("p (q n) -> p q n", q=QUADS)
        grp_back = cst[64:96, C_SEL:C_SEL + C].rearrange("p (k c) -> p k c", k=KC)
        gcr = cst[96:97, C_SEL:C_SEL + 512]
        first_w = cst[:, C_W16:C_W16 + CENT]
        ones = cst[:, C_ONE:C_ONE + P]
        neg_half = cst[:, C_NH:C_NH + 1]
        wqkv = sb("wqkv", [P, KC, 3 * C])
        wproj = sb("wproj", [P, KC, C])
        wf = sb("wf", [P, KC, C])
        wfn = sb("wfn", [P, KC, C])
        wv = sb("wv", [P, KC, C])
        wp = sb("wp", [P, KC, C])
        bvm = sb("bvm", [P, C])
        bfb = sb("bfb", [64, C])
        cols = sb("cols", [P, 16])
        pb_c, bp_c, bf_c = cols[:, 0:3], cols[:, 3:6], cols[:, 6:9]
        nalpha, nbeta = cols[:, 9:10], cols[:, 10:11]
        xs = sb("xs", [P, 2, KC, N])
        xn = sb("xn", [P, KC, N])
        qkn = sb("qkn", [P, 2, 2, N], f32r)
        qs = sb("qs", [P, 2, 2, HPG, 512], f32r)
        ks = sb("ks", [P, 2, HPG, N], f32r)
        vt0 = sb("vt0", [P, 8, C])
        arena = sb("arena", [P, 8192])
        prob = arena[:, 0:6144].rearrange("p (r n) -> p r n", r=6)
        psums = arena[:, 6144:8192].rearrange("p (r n) -> p r n", r=2)
        xn1 = arena[:, 0:3072].rearrange("p (k q n) -> p k q n", k=KC, q=QUADS)
        vt1 = arena[:, 3072:3072 + 8 * VW].rearrange("p (t n) -> p t n", t=8)
        pool1 = arena[:, 3072:3840].rearrange("p (k n) -> p k n", k=KC)
        gmat = arena[:, 6152:6152 + 1536].rearrange("p (k n) -> p k n", k=KC)
        ao = sb("ao", [P, KC, N])
        aof = ao[:, :, :].rearrange("p k n -> p (k n)")
        bdc = aof[:, 0:1536].rearrange("p (k n) -> p k n", k=KC)
        pxn = aof[:, 0:KC * 64].rearrange("p (k n) -> p k n", k=KC)
        sig = aof[:, 0:256]
        eq = aof[:, 256:512]
        wgt = aof[:, 512:768]
        cosb = aof[:, 768:1024]
        simm = aof[:, 1024:1536].rearrange("p (b n) -> p b n", b=2)
        sq = aof[:, 1536:2304].rearrange("p (b n) -> p b n", b=2)
        agg = arena[:, 7688:7688 + C]
        cen = aof[0:64, 2304:2688]
        csq = aof[0:64, 2688:3072]
        mts = aof[:, 2304:2688]
        simt = aof[:, 2688:2944]
        vcx = sb("vcx", [64, VW])
        rden = sb("rden", [P, 512])
        aggt = rden[:, 0:C].rearrange("p (k n) -> p k n", k=KC)
        mx = sb("mx", [P, 2, 16, 2])
        nmx = sb("nmx", [P, 16])
        nmp = sb("nmp", [P, KC, P], f32r)
        st6 = sb("st6", [P, KC, 2, 6])
        mv = sb("mv", [P, KC, 2])
        gst = sb("gst", [P, 8])
        sc0 = sb("sc0", [P, KC, 2])
        sc1 = sb("sc1", [P, KC, 2])
        cn2 = sb("cn2", [64, 2, HEADS1])
        nsq = sb("nsq", [P, 8, HEADS1])
        rn = sb("rn", [P, 8, HEADS1])
        mxs = sb("mxs", [P, 16])
        mw = sb("mw", [P, 16])
        rs = sb("rs", [P, 1])
        bank = [ctx.enter_context(nc.psum_tensor(f"bank{i}", [P, 2 if i in (0, 2) else 1, 512], f32))
                for i in (0, 2, 4, 5, 6, 7)]
        score = [bank[0], bank[1]]
        work = [bank[2][:, 0, :], bank[3][:, 0, :]]
        obank, dbank = bank[4][:, 0, :], bank[5][:, 0, :]
        lb = {0: bank[0][:, 0, :], 1: bank[0][:, 1, :], 2: bank[1][:, 0, :], 3: bank[1][:, 1, :],
              6: obank, 7: dbank}

        const_in = sem("const_in")
        const_done = sem("const_done")
        x_in = sem("x_in")
        score_ready = sem("score_ready")
        exp_done = sem("exp_done")
        pv_done = sem("pv_done")
        sum_done = sem("sum_done")
        den_done = sem("den_done")
        o_copied = sem("o_copied")
        den_copied = sem("den_copied")
        ao_done = sem("ao_done")
        work_ready = sem("work_ready")
        work_free = sem("work_free")
        qk_hi = sem("qk_hi")
        qk_lo = sem("qk_lo")
        stack_in = [sem(f"stack_in{h}") for h in range(HPG)]
        negmax = sem("negmax")
        nm_ready = sem("nm_ready")
        nm_in = sem("nm_in")
        mv_ready = sem("mv_ready")
        var_ready = sem("var_ready")
        rstd_ready = sem("rstd_ready")
        gb_ready = sem("gb_ready")
        sc_ready = sem("sc_ready")
        xn_ready = sem("xn_ready")
        v0_ready = sem("v0_ready")
        l_ready = sem("l_ready")
        l_act = sem("l_act")
        l_dve = sem("l_dve")
        xn1_ready = sem("xn1_ready")
        pxn_ready = sem("pxn_ready")
        cnorm_ready = sem("cnorm_ready")
        crn_ready = sem("crn_ready")
        cen_ready = sem("cen_ready")
        bd_ready = sem("bd_ready")
        sq_used = sem("sq_used")
        norm_ready = sem("norm_ready")
        rn_ready = sem("rn_ready")
        cos_ready = sem("cos_ready")
        sexp_ready = sem("sexp_ready")
        sim_ready = sem("sim_ready")
        agg_ready = sem("agg_ready")
        y_ready = sem("y_ready")
        y_out = sem("y_out")
        chain = sem("chain")
        block = ctx.enter_context(nc.Block())

        PAIRS = samples // 2
        UNIT_TILES = 2 * STEPS

        def quad_view(ap, q):
            f1, f2 = divmod(q, 2)
            v = ap.rearrange("p (y x) -> p y x", y=32)
            return v[:, 16 * f1:16 * f1 + 16, 16 * f2:16 * f2 + 16]

        @block.sync
        def _(sp):
            def stack(n, buf):
                for h in range(HPG):
                    r = slice(32 * h, 32 * h + 32)
                    q_hi, q_lo = qkn[r, 0, 0, :].bitcast(f32), qkn[r, 0, 1, :].bitcast(f32)
                    k_hi, k_lo = qkn[r, 1, 0, :].bitcast(f32), qkn[r, 1, 1, :].bitcast(f32)
                    for row, src in ((0, k_hi), (32, k_hi), (64, k_lo)):
                        sp.dma_start(ks[row:row + 32, buf, h, :].bitcast(f32), src).then_inc(stack_in[h], 16)
                    for row, src in ((0, q_hi), (32, q_lo), (64, q_hi)):
                        sp.dma_start(qs[row:row + 32, buf, :, h, :].bitcast(f32),
                                     src.rearrange("p (a n) -> p a n", a=2)).then_inc(stack_in[h], 16)

            def maxima(buf, half):
                for part in range(2):
                    dst = qs[96 + part:97 + part, buf, half, :, :].bitcast(f32).rearrange("o h n -> o (h n)")
                    sp.dma_start(dst, nmp[0:16, part, :].bitcast(f32)).then_inc(nm_in, 16)

            for k in range(KC):
                sp.dma_start(xs[:, 0, k, :], x[0, k * P:k * P + P, :]).then_inc(x_in, 16)
            sp.dma_start(cst[:, :], consts).then_inc(const_in, 16)
            for t, src in ((wqkv, qkv_t), (wproj, proj_t), (wf, wf_t), (wfn, wf_n), (wv, wv_t), (wp, wp_t)):
                sp.dma_start(t[:, :, :], src.rearrange("(k p) n -> p k n", p=P)).then_inc(const_in, 16)
            for k in range(KC):
                sp.dma_start(xs[:, 1, k, :], x[1, k * P:k * P + P, :]).then_inc(x_in, 16)
            for t, src in ((pb_c, proj_b), (bp_c, bp), (bf_c, bf)):
                for k in range(KC):
                    sp.dma_start(t[:, k:k + 1], src[k * P:k * P + P].rearrange("(p o) -> p o", o=1)).then_inc(const_in, 16)
            sp.dma_start(bvm[:, :], bv.rearrange("(o c) -> o c", o=1).to_broadcast((P, C))).then_inc(const_in, 16)
            for dst, rows in ((bfb[:, :], 64), (aof[96:99, 0:C], 3)):
                sp.dma_start(dst, bf.rearrange("(o c) -> o c", o=1).to_broadcast((rows, C))).then_inc(const_in, 16)
            sp.dma_start(nalpha, alpha.rearrange("(o c) -> o c", o=1).to_broadcast((P, 1))).then_inc(const_in, 16)
            sp.dma_start(nbeta, beta.rearrange("(o c) -> o c", o=1).to_broadcast((P, 1))).then_inc(const_in, 16)

            sp.wait_ge(qk_lo, 8)
            stack(0, 0)
            for half in range(2):
                sp.wait_ge(nm_ready, half + 1)
                maxima(0, half)
            sp.wait_ge(qk_lo, 16)
            stack(1, 1)
            with sp.Fori(0, PAIRS) as it:
                this = [sp.snap(it * 2 + j) for j in range(2)]
                ahead = [sp.snap(it * 2 + (j + 2)) for j in range(2)]
                for j in range(2):
                    def count(per, n):
                        return it * (2 * per) + (j * per + n)
                    for g in range(GROUPS):
                        u = 3 * j + g
                        if g:
                            sp.wait_ge(nm_ready, count(6, 2 * g + 2))
                            maxima(u % 2, 1)
                        sp.wait_ge(nm_ready, count(6, 2 * g + 3))
                        maxima((u + 1) % 2, 0)
                        sp.wait_ge(qk_lo, count(24, 8 * g + 24))
                        stack(u + 2, u % 2)
                    sp.wait_ge(nm_ready, count(6, 8))
                    maxima((3 * j + 3) % 2, 1)
                    sp.wait_ge(y_ready, count(QUADS, QUADS))
                    for k in range(KC):
                        sp.dma_start(y[bass.ds(this[j], 1), k * P:k * P + P, :], xs[:, j, k, :]).then_inc(y_out, 16)
                    sp.wait_ge(y_out, count(16 * KC, 16 * KC))
                    for k in range(KC):
                        sp.dma_start(xs[:, j, k, :], x[bass.ds(ahead[j], 1), k * P:k * P + P, :]).then_inc(x_in, 16)
            sp.wait_ge(x_in, 16 * KC * (samples + 2))
            sp.wait_ge(y_out, 16 * KC * samples)

        @block.tensor
        def _(pe):
            mm = nc.tensor.matmul

            def max_tile(m, buf, out):
                half, h, qt, kh = m // 32, m // 8 % 4, m // 2 % 4, m % 2
                return mm(out, qs[0:96, buf, half, h, qt * P:qt * P + P], ks[0:96, buf, h, kh * 512:kh * 512 + 512],
                          start=True, stop=True)

            def qk_chunk(g, c, out):
                w0 = (c // 4) * C + g * P
                for k in range(KC):
                    last = mm(out[:, 0:256], wqkv[:, k, w0:w0 + P], xn[:, k, (c % 4) * 256:(c % 4) * 256 + 256],
                              start=(k == 0), stop=(k == KC - 1))
                return last

            def value_tile(t, out):
                for k in range(KC):
                    last = mm(out[:, 0:C], xn[:, k, t * P:t * P + P], wqkv[:, k, 2 * C:3 * C],
                              start=(k == 0), stop=(k == KC - 1))
                return last

            def group_stats(out):
                for k in range(KC):
                    last = mm(out[64:96, 0:2], grp_avg[:, k, :], mv[:, k, :], start=(k == 0), stop=(k == KC - 1))
                return last

            def group_back(out):
                for k in range(KC):
                    last = mm(out[:, 2 * k:2 * k + 2], grp_back[:, k, :], gst[64:96, 0:2], start=True, stop=True)
                return last

            def max_rows(out):
                return nc.tensor.transpose(out[0:16, 0:P], nmx[:, :], ident)

            pe.sem_inc(pv_done, 3)
            pe.sem_inc(den_done, 1)
            pe.wait_ge(const_in, 16 * 21)
            pe.wait_ge(const_done, 1)
            for i, (kind, a) in enumerate(PRE_WORK):
                out = work[i % 2]
                pe.wait_ge(work_free, i + 1)
                if kind == "gs1":
                    pe.wait_ge(mv_ready, 1)
                    group_stats(out).then_inc(work_ready, 1)
                elif kind == "gs2":
                    pe.wait_ge(gb_ready, 1)
                    group_back(out).then_inc(work_ready, 1)
                elif kind in ("qk", "qk1"):
                    if a == 0:
                        pe.wait_ge(xn_ready, KC)
                    qk_chunk(kind == "qk1", a, out).then_inc(work_ready, 1)
                elif kind == "v":
                    value_tile(a, out).then_inc(work_ready, 1)
                elif kind == "max":
                    if a in (0, 8, 16, 24):
                        pe.wait_ge(stack_in[a // 8], 96)
                    max_tile(a, 0, out).then_inc(work_ready, 1)
                else:
                    pe.wait_ge(negmax, a + 1)
                    max_rows(out).then_inc(work_ready, 1)

            pe.wait_ge(v0_ready, 8)
            with pe.Fori(0, PAIRS) as it:
                for j in range(2):
                    def count(per, n):
                        return it * (2 * per) + (j * per + n)

                    pe.wait_ge(l_act, count(L1_A, 1 + 0))
                    pe.wait_ge(l_dve, count(L1_D, 1 + 0))
                    done = 0

                    def fill(g, kind, a):
                        nonlocal done
                        i = done
                        done += 1
                        out = work[i % 2]
                        pe.wait_ge(work_free, count(WORK_N, PRE_N + i + 1))
                        if kind == "max":
                            if a in (0, 8, 16, 24):
                                pe.wait_ge(stack_in[a // 8], count(3 * 96, 96 * (g + 2)))
                            max_tile(a, (3 * j + g + 1) % 2, out).then_inc(work_ready, 1)
                        elif kind == "nm":
                            pe.wait_ge(negmax, count(6, 2 * g + 3 if a == 0 else 2 * g + 2))
                            max_rows(out).then_inc(work_ready, 1)
                        elif kind == "qk":
                            if g == 1 and a == 0:
                                pe.wait_ge(xn_ready, count(KC, 2 * KC))
                            qk_chunk((g + 2) % 3, a, out).then_inc(work_ready, 1)
                        elif kind == "gs1":
                            pe.wait_ge(mv_ready, count(2, 2))
                            group_stats(out).then_inc(work_ready, 1)
                        else:
                            pe.wait_ge(gb_ready, count(2, 2))
                            group_back(out).then_inc(work_ready, 1)

                    def denominators(d):
                        if d % 2 == 0:
                            pe.wait_ge(den_copied, count(6, 1 + d // 2))
                        pe.wait_ge(sum_done, count(72, 6 + 6 * (d + 1)))
                        for h in range(HPG):
                            r = slice(32 * h, 32 * h + 32)
                            last = mm(dbank[r, :], ones[:, 0:32],
                                      psums[:, h // 2, (h % 2) * 512:(h % 2) * 512 + 512],
                                      start=(d % 2 == 0), stop=(d % 2 == 1))
                        last.then_inc(den_done, 1)

                    for S in range(GROUPS * STEPS + 1):
                        g, s = divmod(S, STEPS)
                        half, kb = divmod(s, 8)
                        u = 3 * j + g
                        items = list(WORK[S]) if S < len(WORK) else []

                        def work_item():
                            if items:
                                fill(g, *items.pop(0))

                        for p in range(2):
                            if S < GROUPS * STEPS:
                                t = 2 * S + p
                                if kb == 0 and p == 0:
                                    pe.wait_ge(nm_in, count(6 * 32, 32 * (2 * g + half + 1)))
                                pe.wait_ge(exp_done, count(96, t + 1))
                                for e in range(2):
                                    h = 2 * p + e
                                    last = mm(score[p][:, e, :], ks[0:KROWS, u % 2, h, kb * P:kb * P + P],
                                              qs[0:KROWS, u % 2, half, h, :],
                                              start=True, stop=True)
                                last.then_inc(score_ready, 1)
                            work_item()
                        if 1 <= S <= GROUPS * STEPS:
                            T = S - 1
                            tg, tkb = T // STEPS, T % 8
                            if tkb == 0:
                                pe.wait_ge(o_copied, count(6, 1 + T // 8))
                            pe.wait_ge(exp_done, count(96, 2 * T + 4))
                            for h in range(HPG):
                                r = slice(32 * h, 32 * h + 32)
                                last = mm(obank[r, :], vt0[:, tkb, tg * P + 32 * h:tg * P + 32 * h + 32],
                                          prob[:, (2 * T + h // 2) % 6, (h % 2) * 512:(h % 2) * 512 + 512],
                                          start=(tkb == 0), stop=(tkb == 7))
                            last.then_inc(pv_done, 1)
                        work_item()
                        work_item()
                        if S > 4 and S % 4 == 1:
                            denominators((S - 5) // 4)
                        while len(items) > 0:
                            work_item()
                    pe.wait_ge(exp_done, count(96, 98))
                    for n, (kind, a, bk, who) in enumerate(L1):
                        if (kind, a) == ("vp", 2):
                            denominators(11)
                        out = lb[bk]
                        before, freed = freed_before(n)
                        if before == "A":
                            pe.wait_ge(l_act, count(L1_A, 1 + freed))
                        elif before == "D":
                            pe.wait_ge(l_dve, count(L1_D, 1 + freed))
                        if kind == "proj":
                            oc, half = divmod(a, 2)
                            if a == 2:
                                pe.wait_ge(o_copied, count(6, 1 + 6))
                            if a == 3:
                                pe.wait_ge(den_copied, count(6, 1 + 6))
                            pe.wait_ge(ao_done, count(6, 1 + 6))
                            for k in range(KC):
                                last = mm(out, wproj[:, k, oc * P:oc * P + P], ao[:, k, half * 512:half * 512 + 512],
                                          start=(k == 0), stop=(k == KC - 1))
                        elif kind == "vp":
                            last = value_tile(a, out)
                        elif kind == "gs1":
                            pe.wait_ge(mv_ready, count(2, 3))
                            last = group_stats(out)
                        elif kind == "gs2":
                            pe.wait_ge(gb_ready, count(2, 3))
                            last = group_back(out)
                        elif kind in ("cen", "vc"):
                            pe.wait_ge(pxn_ready, count(1, 1))
                            w = wf if kind == "cen" else wv
                            for k in range(KC):
                                last = mm(out[0:64, 0:C], pxn[:, k, :], w[:, k, :], start=(k == 0), stop=(k == KC - 1))
                        elif kind in ("f", "v"):
                            q, hf = divmod(a, 2)
                            if kind == "f" and a in (0, 4):
                                pe.wait_ge(xn1_ready, count(2, 1 + a // 4))
                            w = wf if kind == "f" else wv
                            for k in range(KC):
                                last = mm(out[:, 0:C], xn1[:, k, q, hf * P:hf * P + P], w[:, k, :],
                                          start=(k == 0), stop=(kind == "v" and k == KC - 1))
                            if kind == "f":
                                last = mm(out[:, 0:C], ks[96:99, 0, 0, 0:P], nmp[96:99, :, :].rearrange("p k n -> p (k n)"), start=False, stop=True)
                        elif kind == "cenT":
                            pe.wait_ge(cen_ready, count(1, 1))
                            for k in range(KC):
                                last = mm(out[:, 64 * k:64 * k + 64], cen[:, k * P:k * P + P], ident[0:64, 0:64],
                                          start=True, stop=True)
                        elif kind == "gc":
                            pe.wait_ge(bd_ready, count(1, 1))
                            for k in range(KC):
                                last = mm(out[96:97, :], bf_c[:, k:k + 1], bdc[:, k, :], start=(k == 0), stop=(k == KC - 1))
                        elif kind == "G":
                            for k in range(KC):
                                last = mm(out, wfn[:, k, a * P:a * P + P], bdc[:, k, :], start=(k == 0), stop=(k == KC - 1))
                        elif kind == "num":
                            if a == 0:
                                pe.wait_ge(l_act, count(L1_A, 1 + act_items("G", 2)))
                                pe.wait_ge(l_dve, count(L1_D, 1 + sum(w == "D" for _, _, _, w in L1[:L1_AT["gc", 0] + 1])))
                            for hf in range(2):
                                o = out[:, hf * P:hf * P + P]
                                for k in range(KC):
                                    mm(o, xn1[:, k, a, hf * P:hf * P + P], gmat[:, k, a * P:a * P + P],
                                       start=(k == 0), stop=False)
                                last = mm(o, ones[96:97, :], gcr[:, a * P:a * P + P], start=False, stop=True)
                        elif kind == "agg":
                            pe.wait_ge(sim_ready, count(QUADS, a + 1))
                            for hf in range(2):
                                mm(out[:, 0:VW], simm[:, a % 2, hf * P:hf * P + P], vt1[:, 2 * a + hf, :],
                                   start=(hf == 0), stop=False)
                            last = mm(out[:, 0:VW], sel_q[:, a, :], vcx[:, :], start=False, stop=True)
                        elif kind == "sT":
                            for hf in range(2):
                                last = nc.tensor.transpose(out[:, hf * P:hf * P + P], simm[:, a % 2, hf * P:hf * P + P], ident)
                        elif kind == "aT":
                            pe.wait_ge(agg_ready, count(QUADS, a + 1))
                            for k in range(KC):
                                last = nc.tensor.transpose(out[:, k * P:k * P + P], agg[:, k * P:k * P + P], ident)
                        elif kind == "MT":
                            pe.wait_ge(l_act, count(L1_A, 1 + act_items("aT", a)))
                            for k in range(KC):
                                last = mm(out[:, 0:C], aggt[:, k, :], wp[:, k, :], start=(k == 0), stop=(k == KC - 1))
                        elif kind in ("outa", "outb"):
                            pe.wait_ge(l_act, count(L1_A, 1 + act_items("MT", a)))
                            for e, oc in enumerate((0, 1) if kind == "outa" else (2,)):
                                last = mm(out[:, e * QT:e * QT + QT], mts[:, oc * P:oc * P + P], simt, start=True, stop=True)
                        last.then_inc(l_ready, 1)
                        for kind, a in LATE_WORK.get((kind, a), ()):
                            fill(3 if kind == "nm" else 2, kind, a)

        @block.scalar
        def _(act):
            def norm0(slot, k):
                return nc.scalar.activation(xn[:, k, :], xs[:, slot, k, :], ACT.Identity,
                                            bias=sc0[:, k, 1:2], scale=sc0[:, k, 0:1])

            act.sem_inc(exp_done, 2)
            act.sem_inc(o_copied, 1)
            act.sem_inc(den_copied, 1)
            act.sem_inc(l_act, 1)
            act.wait_ge(sc_ready, 1)
            for k in range(KC):
                norm0(0, k).then_inc(xn_ready, 1)
            for i, (kind, a) in enumerate(PRE_WORK):
                if kind in ("qk", "qk1"):
                    if kind == "qk1" and a == 0:
                        for h in range(HPG):
                            act.wait_ge(stack_in[h], 96)
                    act.wait_ge(work_ready, i + 1)
                    nc.scalar.activation(qkn[:, a // 4, 0, (a % 4) * 256:(a % 4) * 256 + 256], work[i % 2][:, 0:256],
                                         ACT.Copy).then_inc(qk_hi, 1)

            with act.Fori(0, PAIRS) as it:
                for j in range(2):
                    def count(per, n):
                        return it * (2 * per) + (j * per + n)
                    done = 0

                    def copy_denominators(H):
                        act.wait_ge(den_done, count(12, 1 + 2 * H + 2))
                        act.wait_ge(ao_done, count(6, 1 + H))
                        nc.scalar.activation(rden[:, :], dbank, ACT.Copy).then_inc(den_copied, 1)

                    for S in range(GROUPS * STEPS + 1):
                        g, s = divmod(S, STEPS)
                        if S < GROUPS * STEPS:
                            for p in range(2):
                                t = 2 * S + p
                                act.wait_ge(score_ready, count(96, t + 1))
                                act.wait_ge(pv_done, count(48, S + 1))
                                act.wait_ge(sum_done, count(72, 6 + sums(S - 3, p)))
                                nc.scalar.activation(prob[:, t % 6, :], score[p][:, :, :].rearrange("p e n -> p (e n)"),
                                                     ACT.Exp, scale=SCALE0).then_inc(exp_done, 1)
                                if p == 0 and S % 8 == 1 and S > 8:
                                    H = S // 8 - 1
                                    act.wait_ge(pv_done, count(48, 3 + 8 * (H + 1)))
                                    nc.scalar.activation(ao[:, H // 2, (H % 2) * 512:(H % 2) * 512 + 512], obank,
                                                         ACT.Copy).then_inc(o_copied, 1)
                                if p == 0 and S % 8 == 2 and S > 8:
                                    copy_denominators(S // 8 - 1)
                        else:
                            act.wait_ge(pv_done, count(48, 3 + 48))
                            nc.scalar.activation(ao[:, 2, 512:1024], obank, ACT.Copy).then_inc(o_copied, 1)
                        for kind, a in WORK[S]:
                            if kind == "qk":
                                if a == 0:
                                    for h in range(HPG):
                                        act.wait_ge(stack_in[h], count(3 * 96, 96 * (g + 2)))
                                act.wait_ge(work_ready, count(WORK_N, PRE_N + done + 1))
                                nc.scalar.activation(qkn[:, a // 4, 0, (a % 4) * 256:(a % 4) * 256 + 256],
                                                     work[done % 2][:, 0:256], ACT.Copy).then_inc(qk_hi, 1)
                                if g == 0 and a == 7:
                                    qk_end = done
                            done += 1
                        if S in (17, 18, 19):
                            if S == 17:
                                act.wait_ge(sc_ready, count(2, 2))
                                act.wait_ge(work_ready, count(WORK_N, PRE_N + qk_end + 1))
                            norm0(1 - j, S - 17).then_inc(xn_ready, 1)

                    def item(kind, a):
                        n = L1_AT[kind, a]
                        act.wait_ge(l_ready, count(L1_N, n + 1))
                        return lb[L1[n][2]]

                    def value_copy(a):
                        nc.scalar.activation(vt0[:, a, :], item("vp", a)[:, 0:C], ACT.Copy).then_inc(l_act, 1)
                    for a in range(7):
                        if a == 2:
                            copy_denominators(5)
                        value_copy(a)
                    act.wait_ge(sc_ready, count(2, 3))
                    for f1 in range(2):
                        for k in range(KC):
                            src = xs[:, j, k, 512 * f1:512 * f1 + 512].rearrange("p (y f x) -> p f y x", y=16, f=2)
                            dst = xn1[:, k, 2 * f1:2 * f1 + 2, :].rearrange("p f (y x) -> p f y x", y=16)
                            last = nc.scalar.activation(dst, src, ACT.Identity, bias=sc1[:, k, 1:2], scale=sc1[:, k, 0:1])
                        last.then_inc(xn1_ready, 1)
                    value_copy(7)

                    def sim_exp(q):
                        act.wait_ge(cos_ready, count(QUADS, q + 1))
                        nc.scalar.activation(cosb, cosb, ACT.Exp, bias=nbeta, scale=nalpha).then_inc(sexp_ready, 1)

                    exps = {("f", 4): 0, ("aT", 0): 1, ("f", 7): 2, ("sT", 2): 3}
                    for kind, a, _, who in L1[L1_AT["f", 0]:]:
                        if (kind, a) in exps:
                            sim_exp(exps[kind, a])
                        if who == "A":
                            out = item(kind, a)
                            if kind == "f":
                                act.wait_ge(sq_used, count(8, a + 1))
                                nc.scalar.activation(sq[:, a % 2, :], out[:, 0:C], ACT.Square).then_inc(l_act, 1)
                            elif kind == "vc":
                                nc.scalar.activation(vcx[:, 0:C], out[0:64, 0:C], ACT.Copy).then_inc(l_act, 1)
                            elif kind == "G":
                                nc.scalar.activation(gmat[:, a, :], out, ACT.Copy).then_inc(l_act, 1)
                            elif kind == "sT":
                                nc.scalar.activation(simt, out[:, 0:QT], ACT.Copy).then_inc(l_act, 1)
                            elif kind == "aT":
                                nc.scalar.activation(aggt.rearrange("p k n -> p (k n)"), out[:, 0:C], ACT.Copy).then_inc(l_act, 1)
                            else:
                                nc.scalar.activation(mts, out[:, 0:C], ACT.Copy).then_inc(l_act, 1)

        @block.vector
        def _(dve):
            v = nc.vector
            linked = [0]
            base = [0]

            def link(ins):
                linked[0] += 1
                ins.then_inc(chain, 1)
                dve.wait_ge(chain, base[0] + linked[0])

            def channel_stats(slot, k, half):
                v.bn_stats(st6[:, k, half, :], xs[:, slot, k, half * 512:half * 512 + 512])

            def channel_moments():
                for k in range(KC):
                    last = v.bn_aggr(mv[:, k, :], st6[:, k, :, :])
                link(last)
                link(v.tensor_tensor(mxs[:, 0:KC], mv[:, :, 0], mv[:, :, 0], ALU.mult))
                v.tensor_tensor(mv[:, :, 1], mv[:, :, 1], mxs[:, 0:KC], ALU.add).then_inc(mv_ready, 1)

            G = slice(64, 96)
            g_scale, g_shift, g_mean, g_sq, g_var = (gst[G, i:i + 1] for i in range(5))

            def group_variance():
                link(v.scalar_tensor_tensor(out=g_var, in0=g_mean, scalar=g_mean, in1=g_sq, op0=ALU.mult, op1=ALU.subtract))
                v.tensor_scalar(g_var, g_var, -1.0, GN_EPS, ALU.mult, ALU.add).then_inc(var_ready, 1)

            def group_shift():
                v.scalar_tensor_tensor(out=g_shift, in0=g_mean, scalar=-1.0, in1=g_scale,
                                       op0=ALU.mult, op1=ALU.mult).then_inc(gb_ready, 1)

            def max_item(m, out):
                i = m // 2 % 16
                v.tensor_reduce(mx[:, m // 32, i, m % 2:m % 2 + 1], out, AX.X, ALU.max).then_inc(work_free, 1)

            def negated_maxima(half):
                v.tensor_reduce(nmx[:, :], mx[:, half, :, :], AX.X, ALU.max, negate=True).then_inc(negmax, 1)

            def maxima_parts(out):
                link(v.tensor_copy(nmp[0:16, 0, :], out[0:16, 0:P]))
                v.tensor_tensor(nmp[0:16, 1, :], out[0:16, 0:P], nmp[0:16, 0, :].bitcast(f32), ALU.subtract).then_inc(nm_ready, 1)

            def low_part(a, out):
                r = slice((a % 4) * 256, (a % 4) * 256 + 256)
                v.tensor_tensor(qkn[:, a // 4, 1, r], out[:, 0:256], qkn[:, a // 4, 0, r].bitcast(f32), ALU.subtract).then_inc(qk_lo, 1)

            dve.sem_inc(work_free, 2)
            dve.sem_inc(sq_used, 2)
            dve.sem_inc(ao_done, 1)
            dve.sem_inc(l_dve, 1)
            for b in range(2):
                v.memset(ks[96:99, b, :, :].bitcast(f32), 1.0)
            dve.wait_ge(const_in, 16 * 21)
            link(v.tensor_scalar(cols[:, 9:11], cols[:, 9:11], -1.0, None, ALU.mult))
            R = slice(96, 99)
            part = [aof[R, (i + 1) * C:(i + 2) * C].bitcast(f32r) for i in range(3)]
            whole, rest, total = (aof[R, i * C:(i + 1) * C] for i in (0, 4, 5))
            link(v.tensor_copy(part[0], whole))
            link(v.tensor_tensor(rest, whole, part[0].bitcast(f32), ALU.subtract))
            link(v.tensor_copy(part[1], rest))
            link(v.tensor_tensor(part[2], rest, part[1].bitcast(f32), ALU.subtract))
            link(v.tensor_scalar(total, part[0].bitcast(f32), ident[R, 96:97], None, ALU.mult))
            link(v.scalar_tensor_tensor(out=total, in0=part[1].bitcast(f32), scalar=ident[R, 97:98], in1=total,
                                        op0=ALU.mult, op1=ALU.add))
            link(v.scalar_tensor_tensor(out=nmp[R, :, :].rearrange("p k n -> p (k n)"), in0=part[2].bitcast(f32), scalar=ident[R, 98:99],
                                        in1=total, op0=ALU.mult, op1=ALU.add))
            v.tensor_tensor(bvm[:, :], bvm[:, :], mask_hm, ALU.mult).then_inc(const_done, 1)

            dve.wait_ge(x_in, 16 * KC)
            for k in range(KC):
                for half in range(2):
                    last = v.bn_stats(st6[:, k, half, :], xs[:, 0, k, half * 512:half * 512 + 512])
            link(last)
            channel_moments()
            for i, (kind, a) in enumerate(PRE_WORK):
                out = work[i % 2]
                if kind == "max":
                    dve.wait_ge(work_ready, i + 1)
                    max_item(a, out)
                    if a in (31, 63):
                        dve.wait_ge(work_free, 2 + i + 1)
                        negated_maxima(a // 32)
                elif kind == "nm":
                    dve.wait_ge(work_ready, i + 1)
                    dve.wait_ge(nm_in, 32 * a)
                    maxima_parts(out)
                    dve.wait_ge(nm_ready, a + 1)
                    dve.sem_inc(work_free, 1)
                elif kind in ("qk", "qk1"):
                    dve.wait_ge(qk_hi, (8 if kind == "qk1" else 0) + a + 1)
                    low_part(a, out)
                    dve.wait_ge(qk_lo, (8 if kind == "qk1" else 0) + a + 1)
                    dve.sem_inc(work_free, 1)
                elif kind == "v":
                    dve.wait_ge(work_ready, i + 1)
                    link(v.tensor_copy(vt0[:, a, :], out[:, 0:C]))
                    dve.sem_inc(work_free, 1)
                    dve.sem_inc(v0_ready, 1)
                elif kind == "gs1":
                    dve.wait_ge(work_ready, i + 1)
                    link(v.tensor_copy(gst[G, 2:4], out[G, 0:2]))
                    dve.sem_inc(work_free, 1)
                    group_variance()
                    dve.wait_ge(rstd_ready, 1)
                    group_shift()
                else:
                    dve.wait_ge(work_ready, i + 1)
                    link(v.tensor_copy(sc0[:, :, :].rearrange("p k n -> p (k n)"), out[:, 0:6]))
                    dve.sem_inc(work_free, 1)
                    dve.sem_inc(sc_ready, 1)
            pre_links = linked[0]

            with dve.Fori(0, PAIRS) as it:
                base[0] = it * CHAIN_PAIR
                for j in range(2):
                    def count(per, n):
                        return it * (2 * per) + (j * per + n)
                    done = 0

                    def released(ins):
                        ins.then_inc(work_free, 1)
                        dve.wait_ge(work_free, count(WORK_N, PRE_N + 2 + done + 1))

                    def use(g, kind, a):
                        nonlocal done
                        out = work[done % 2]
                        if kind != "qk":
                            dve.wait_ge(work_ready, count(WORK_N, PRE_N + done + 1))
                        if kind == "max":
                            max_item(a, out)
                            if a in (31, 63):
                                dve.wait_ge(work_free, count(WORK_N, PRE_N + 2 + done + 1))
                                negated_maxima(a // 32)
                        elif kind == "nm":
                            n = 2 * g + 3 if a == 0 else 2 * g + 2
                            dve.wait_ge(nm_in, count(6 * 32, 32 * (n - 1)))
                            maxima_parts(out)
                            dve.wait_ge(nm_ready, count(6, n))
                            dve.sem_inc(work_free, 1)
                        elif kind == "qk":
                            dve.wait_ge(qk_hi, count(24, 16 + 8 * g + a + 1))
                            low_part(a, out)
                            dve.wait_ge(qk_lo, count(24, 16 + 8 * g + a + 1))
                            dve.sem_inc(work_free, 1)
                        elif kind == "gs1":
                            released(v.tensor_copy(gst[G, 2:4], out[G, 0:2]))
                            group_variance()
                        else:
                            released(v.tensor_copy(sc0[:, :, :].rearrange("p k n -> p (k n)"), out[:, 0:6]))
                            dve.sem_inc(sc_ready, 1)
                        done += 1

                    def late(kind, a=0):
                        for what, m in LATE_WORK.get((kind, a), ()):
                            use(3 if what == "nm" else 2, what, m)

                    def denominators_part(H, i):
                        if i == 0:
                            dve.wait_ge(den_copied, count(6, 1 + H + 1))
                        r = rden[:, i * P:i * P + P]
                        ins = v.reciprocal(r, r)
                        if i == 3:
                            link(ins)
                            o = ao[:, H // 2, (H % 2) * 512:(H % 2) * 512 + 512]
                            v.tensor_tensor(o, o, rden[:, :], ALU.mult).then_inc(ao_done, 1)

                    for S in range(GROUPS * STEPS + 1):
                        g = S // STEPS
                        b = S - 4
                        if b == 0:
                            dve.wait_ge(x_in, count(16 * KC, 32 * KC))
                        if 0 <= b < 6:
                            last = v.bn_stats(st6[:, b // 2, b % 2, :], xs[:, 1 - j, b // 2, (b % 2) * 512:(b % 2) * 512 + 512])
                            if b == 5:
                                link(last)
                        if S == 13:
                            dve.wait_ge(rstd_ready, count(2, 2))
                            group_shift()
                        for kind, a in WORK[S]:
                            use(g, kind, a)
                        if b == 5:
                            channel_moments()
                        if S > 10 and 3 <= S % 8 <= 6:
                            denominators_part(S // 8 - 1, S % 8 - 3)
                    late("vp", 0)
                    late("vp", 1)
                    late("vp", 2)
                    denominators_part(5, 0)
                    late("vp", 3)
                    denominators_part(5, 1)
                    late("vp", 4)
                    denominators_part(5, 2)
                    denominators_part(5, 3)

                    freed = [0]

                    def item(kind, a=0):
                        n = L1_AT[kind, a]
                        assert sum(w == "D" for _, _, _, w in L1[:n]) == freed[0], (kind, a)
                        dve.wait_ge(l_ready, count(L1_N, n + 1))
                        return lb[L1[n][2]]

                    def read(ins, then=False):
                        freed[0] += 1
                        ins.then_inc(l_dve, 1)
                        if then:
                            dve.wait_ge(l_dve, count(L1_D, 1 + freed[0]))

                    for i in range(6):
                        oc, half = divmod(i, 2)
                        o = xs[:, j, oc, half * 512:half * 512 + 512]
                        read(v.scalar_tensor_tensor(out=o, in0=item("proj", i), scalar=pb_c[:, oc:oc + 1], in1=o,
                                                    op0=ALU.add, op1=ALU.add), then=True)
                        last = v.bn_stats(st6[:, oc, half, :], o)
                        if i < 5:
                            late("proj", i)
                    link(last)
                    v.memset(vcx[:, C:VW], 1.0)
                    channel_moments()

                    def pool_rows(k):
                        return v.tensor_reduce(pool1[:, k, :], xs[:, j, k, :].rearrange("p (n i) -> p n i", i=4), AX.X, ALU.add)
                    late("proj", 5)
                    read(v.tensor_copy(gst[G, 2:4], item("gs1")[G, 0:2]), then=True)
                    group_variance()
                    pool_rows(0)
                    dve.wait_ge(rstd_ready, count(2, 3))
                    group_shift()
                    late("gs1")
                    pool_rows(1)
                    read(v.tensor_copy(sc1[:, :, :].rearrange("p k n -> p (k n)"), item("gs2")[:, 0:6]), then=True)
                    dve.sem_inc(sc_ready, 1)
                    late("gs2")
                    link(pool_rows(2))
                    for k in range(KC):
                        for f1 in range(2):
                            src = pool1[:, k, 128 * f1:128 * f1 + 128].rearrange("p (w i f h) -> p f w h i", w=4, i=4, f=2)
                            dst = pxn[:, k, 32 * f1:32 * f1 + 32].rearrange("p (f w h) -> p f w h", f=2, w=4)
                            last = v.tensor_reduce(dst, src, AX.X, ALU.add)
                    link(last)
                    link(v.tensor_scalar(pxn[:, :, :], pxn[:, :, :], 1.0 / 16, None, ALU.mult))
                    for k in range(KC):
                        last = v.tensor_scalar(pxn[:, k, :], pxn[:, k, :], sc1[:, k, 0:1], sc1[:, k, 1:2], ALU.mult, ALU.add)
                    last.then_inc(pxn_ready, 1)
                    v.memset(vt1[:, :, C:VW], 1.0)

                    def tile_values(t):
                        read(v.tensor_copy(vt1[:, t, 0:C], item("v", t)[:, 0:C]))

                    def tile_norms(t):
                        dve.wait_ge(l_act, count(L1_A, 1 + act_items("f", t)))
                        v.tensor_reduce(nsq[:, t, :], sq[:, t % 2, :].rearrange("p (h d) -> p h d", h=HEADS1),
                                        AX.X, ALU.add).then_inc(sq_used, 1)

                    def tile(t):
                        late("f", t)
                        tile_values(t)
                        tile_norms(t)
                        late("v", t)
                        if t % 2:
                            dve.wait_ge(sq_used, count(8, 2 + t + 1))
                            v.tensor_scalar(nsq[:, t - 1:t + 1, :], nsq[:, t - 1:t + 1, :], NORM_EPS2, None,
                                            ALU.max).then_inc(norm_ready, 1)

                    tile(0)
                    read(v.tensor_tensor(cen, item("cen")[0:64, 0:C], bfb[:, :], ALU.add), then=True)
                    link(v.tensor_tensor(csq, cen, cen, ALU.mult))
                    link(v.tensor_reduce(cn2[:, 0, :], csq.rearrange("p (h d) -> p h d", h=HEADS1), AX.X, ALU.add))
                    v.tensor_scalar(cn2[:, 0, :], cn2[:, 0, :], NORM_EPS2, None, ALU.max).then_inc(cnorm_ready, 1)

                    late("vc")
                    dve.wait_ge(crn_ready, count(1, 1))
                    v.tensor_tensor(cen.rearrange("p (h d) -> p h d", h=HEADS1), cen.rearrange("p (h d) -> p h d", h=HEADS1),
                                    cn2[:, 1, :].unsqueeze(2).to_broadcast((64, HEADS1, DH1)), ALU.mult).then_inc(cen_ready, 1)
                    def first_tiles():
                        for t in range(1, 4):
                            tile(t)
                            if t == 1:
                                diagonal_centres()
                            if t == 2:
                                read(v.tensor_copy(gcr, item("gc")[96:97, :]))

                    def diagonal_centres():
                        out = item("cenT")
                        for k in range(KC):
                            ins = v.tensor_tensor(
                                bdc[:, k, :].rearrange("p (q h m) -> p q h m", q=QUADS, h=HEADS1),
                                out[:, 64 * k:64 * k + 64].rearrange("p (q m) -> p q m", q=QUADS).unsqueeze(2)
                                   .to_broadcast((P, QUADS, HEADS1, CENT)),
                                mask_d[:, k, :].unsqueeze(1).unsqueeze(3).to_broadcast((P, QUADS, HEADS1, CENT)), ALU.mult)
                        read(ins, then=True)
                        dve.sem_inc(bd_ready, 1)

                    first_tiles()

                    def hmview(ap):
                        return ap.rearrange("p (t m) -> p t m", m=CENT)

                    def over_centres(ap):
                        return ap.unsqueeze(2).to_broadcast((P, 2 * HEADS1, CENT))

                    def cosines(q):
                        dve.wait_ge(rn_ready, count(QUADS, q + 1))
                        read(v.tensor_tensor(hmview(cosb), hmview(item("num", q)[:, 0:QT]),
                                             over_centres(rn[:, 2 * q:2 * q + 2, :].rearrange("p t h -> p (t h)")), ALU.mult), then=True)
                        dve.sem_inc(cos_ready, 1)

                    def sigmoids(q):
                        dve.wait_ge(sexp_ready, count(QUADS, q + 1))
                        link(v.tensor_scalar(cosb, cosb, 1.0, None, ALU.add))
                        link(v.reciprocal(sig, cosb))

                    def only_first_largest(q):
                        link(v.tensor_reduce(mxs[:, :], hmview(sig), AX.X, ALU.max))
                        link(v.tensor_tensor(hmview(eq), hmview(sig), over_centres(mxs[:, :]), ALU.is_equal))
                        link(v.tensor_tensor(hmview(wgt), hmview(eq),
                                             first_w.unsqueeze(1).to_broadcast((P, 2 * HEADS1, CENT)), ALU.mult))
                        link(v.tensor_reduce(mw[:, :], hmview(wgt), AX.X, ALU.max))
                        link(v.tensor_tensor(hmview(eq), hmview(wgt), over_centres(mw[:, :]), ALU.is_equal))
                        if q >= 2:
                            dve.wait_ge(l_ready, count(L1_N, L1_AT["sT", q - 2] + 1))
                        v.tensor_tensor(simm[:, q % 2, :], eq, sig, ALU.mult).then_inc(sim_ready, 1)

                    def aggregates(q):
                        out = item("agg", q)
                        link(v.reciprocal(rs[:, :], out[:, C:VW]))
                        read(v.scalar_tensor_tensor(out=agg, in0=out[:, 0:C], scalar=rs[:, :], in1=mask_hm,
                                                    op0=ALU.mult, op1=ALU.mult), then=True)
                        v.tensor_tensor(agg, agg, bvm[:, :], ALU.add).then_inc(agg_ready, 1)

                    def outputs(q):
                        for kind, ocs in (("outa", (0, 1)), ("outb", (2,))):
                            out = item(kind, q)
                            for e, oc in enumerate(ocs):
                                o = quad_view(xs[:, j, oc, :], q)
                                ins = v.scalar_tensor_tensor(out=o, in0=out[:, e * QT:e * QT + QT].rearrange("p (y x) -> p y x", y=16),
                                                             scalar=bp_c[:, oc:oc + 1], in1=o, op0=ALU.add, op1=ALU.add)
                            read(ins, then=(kind == "outb"))
                        dve.sem_inc(y_ready, 1)

                    cosines(0)
                    sigmoids(0)
                    only_first_largest(0)
                    tile(4)
                    aggregates(0)
                    cosines(1)
                    sigmoids(1)
                    only_first_largest(1)
                    tile(5)
                    tile(6)
                    aggregates(1)
                    outputs(0)
                    cosines(2)
                    sigmoids(2)
                    only_first_largest(2)
                    tile(7)
                    aggregates(2)
                    outputs(1)
                    cosines(3)
                    sigmoids(3)
                    only_first_largest(3)
                    aggregates(3)
                    outputs(2)
                    outputs(3)
                assert linked[0] == pre_links + CHAIN_PAIR, (linked[0], pre_links)

        @block.gpsimd
        def _(pool):
            pool.sem_inc(sum_done, 6)
            pool.wait_ge(const_in, 16 * 21)
            pool.wait_ge(var_ready, 1)
            nc.gpsimd.tensor_tensor(gst[64:96, 0:1], gst[64:96, 4:5], neg_half[64:96, :], ALU.pow).then_inc(rstd_ready, 1)
            with pool.Fori(0, PAIRS) as it:
                for j in range(2):
                    def count(per, n):
                        return it * (2 * per) + (j * per + n)
                    for S in range(GROUPS * STEPS):
                        if S % 4 == 0:
                            continue
                        for p in range(2):
                            pool.wait_ge(exp_done, count(96, 2 + 2 * S + p + 1))
                            if S % 4 == 1:
                                pool.wait_ge(den_done, count(12, 1 + S // 4))
                                so_far = prob[:, (2 * S - 2 + p) % 6, :]
                            else:
                                pool.wait_ge(sum_done, count(72, 6 + sums(S - 1, p)))
                                so_far = psums[:, p, :]
                            nc.gpsimd.tensor_tensor(psums[:, p, :], so_far, prob[:, (2 * S + p) % 6, :],
                                                    ALU.add).then_inc(sum_done, 1)
                        if S == 11:
                            pool.wait_ge(var_ready, count(2, 2))
                            pool.wait_ge(sum_done, count(72, 6 + sums(S, 1)))
                            nc.gpsimd.tensor_tensor(gst[64:96, 0:1], gst[64:96, 4:5], neg_half[64:96, :],
                                                    ALU.pow).then_inc(rstd_ready, 1)
                            pool.wait_ge(rstd_ready, count(2, 2))
                    pool.wait_ge(var_ready, count(2, 3))
                    pool.wait_ge(sum_done, count(72, 6 + 72))
                    nc.gpsimd.tensor_tensor(gst[64:96, 0:1], gst[64:96, 4:5], neg_half[64:96, :],
                                            ALU.pow).then_inc(rstd_ready, 1)
                    pool.wait_ge(rstd_ready, count(2, 3))
                    pool.wait_ge(cnorm_ready, count(1, 1))
                    nc.gpsimd.tensor_tensor(cn2[:, 1, :], cn2[:, 0, :], neg_half[0:64, :].to_broadcast((64, HEADS1)),
                                            ALU.pow).then_inc(crn_ready, 1)
                    for q in range(QUADS):
                        pool.wait_ge(norm_ready, count(QUADS, q + 1))
                        nc.gpsimd.tensor_tensor(rn[:, 2 * q:2 * q + 2, :].rearrange("p t h -> p (t h)"),
                                                nsq[:, 2 * q:2 * q + 2, :].rearrange("p t h -> p (t h)"),
                                                neg_half.to_broadcast((P, 2 * HEADS1)), ALU.pow).then_inc(rn_ready, 1)


CHAIN_PAIR = 114
SAMPLES = 16


def constants():
    import numpy as np
    c = np.zeros((P, C_COLS), np.float32)
    c[:, C_ID:C_ID + P] = np.eye(P)
    ch = np.arange(C)
    size = C // GN_GROUPS
    for k in range(KC):
        for p in range(P):
            c[p, C_GA + k * 32 + (k * P + p) // size] = 1.0 / size
            c[p, C_MD + k * HEADS1 + (k * P + p) // DH1] = 1.0
    hm = np.arange(P)
    c[:, C_BD:C_BD + C] = hm[:, None] // CENT == ch[None, :] // DH1
    for q in range(QUADS):
        for m in range(CENT):
            c[q * CENT + m, C_SEL + q * P + m:C_SEL + (q + 1) * P:CENT] = 1.0
    c[64:96, C_SEL:C_SEL + C] = ch[None, :] // size == np.arange(GN_GROUPS)[:, None]
    c[:, C_W16:C_W16 + CENT] = CENT - np.arange(CENT)
    c[:, C_ONE:C_ONE + P] = 1.0
    c[:, C_NH] = -0.5
    return c


def kernel(x, L0_conv_qkv_w, L0_conv_proj_w, L0_conv_proj_b, L1_conv_Wf, L1_conv_bf, L1_conv_Wv, L1_conv_bv,
           L1_conv_Wp, L1_conv_bp, L1_conv_sim_alpha, L1_conv_sim_beta):
    import concourse.bacc as bacc
    import numpy as np
    from concourse.bass_utils import run_bass_kernel_spmd

    x = np.asarray(x)
    samples = x.shape[0]
    tokens = x.reshape(samples, C, N)
    a = np.ascontiguousarray
    arrays = {
        "x": np.concatenate([tokens, tokens[:2]]),
        "qkv_t": a(np.asarray(L0_conv_qkv_w).T), "proj_t": a(np.asarray(L0_conv_proj_w).T),
        "proj_b": np.asarray(L0_conv_proj_b), "wf_t": a(np.asarray(L1_conv_Wf).T), "wf_n": np.asarray(L1_conv_Wf),
        "bf": np.asarray(L1_conv_bf), "wv_t": a(np.asarray(L1_conv_Wv).T), "bv": np.asarray(L1_conv_bv),
        "wp_t": a(np.asarray(L1_conv_Wp).T), "bp": np.asarray(L1_conv_bp),
        "alpha": np.asarray(L1_conv_sim_alpha), "beta": np.asarray(L1_conv_sim_beta), "consts": constants(),
    }
    nc = bacc.Bacc("TRN2", target_bir_lowering=False, num_devices=1, dynamic_dma_scratch_size=1024)
    args = [nc.dram_tensor(n, v.shape, mybir.dt.float32, kind="ExternalInput").ap() for n, v in arrays.items()]
    y = nc.dram_tensor("y", (samples, C, N), mybir.dt.float32, kind="ExternalOutput").ap()
    conv_kernel(nc, samples, *args, y)
    got = run_bass_kernel_spmd(nc, [arrays], core_ids=[0])
    return got.results[0]["y"].reshape(samples, C, 32, 32)
```
